# Optimizing a Trainium2 kernel written in Bass

```python
import numpy as np
import jax
import jax.numpy as jnp

def _softmax(x, axis=-1):
    return jax.nn.softmax(x, axis=axis)

def _gelu(x):
    return jax.nn.gelu(x, approximate=True)

def _silu(x):
    return jax.nn.silu(x)

def _sigmoid(x):
    return jax.nn.sigmoid(x)

def _layernorm(x, axis=-1, eps=1e-05):
    m = jnp.mean(x, axis=axis, keepdims=True)
    v = jnp.var(x, axis=axis, keepdims=True)
    return (x - m) / jnp.sqrt(v + eps)

def _scatter_add(tgt, idx, src, axis=0):
    return tgt.at[idx].add(src)

def _segment_sum(src, seg, n):
    return jax.ops.segment_sum(src, seg, n)
kernel_name = 'mk_recurrent_d1_jaxref_r4_b4a310'

def setup_inputs(seed: int=0):
    np.random.seed(seed)
    _w = jnp.asarray

    def _L0_attn_setup():
        import jax, jax.numpy as jnp
        import numpy as np
        import math
        D_MODEL = 512
        NUM_HEADS = 16
        D_K = D_MODEL // NUM_HEADS
        SEQ_LEN = 512
        THETA = 10000.0
        BATCH = 2

        def _rope(t):
            S = t.shape[-2]
            dk = t.shape[-1]
            inv_freq = jnp.exp(-math.log(THETA) * jnp.arange(0, dk, 2, dtype=jnp.float32) / dk)
            pos = jnp.arange(S, dtype=jnp.float32)
            freqs = pos[:, None] * inv_freq[None, :]
            cos = jnp.cos(freqs)
            sin = jnp.sin(freqs)
            t1 = t[..., ::2]
            t2 = t[..., 1::2]
            rot = jnp.stack([t1 * cos - t2 * sin, t1 * sin + t2 * cos], axis=-1)
            return rot.reshape(t.shape)
        key = jax.random.key(seed)
        ks = jax.random.split(key, 5)
        std = (2.0 / (D_MODEL + D_MODEL)) ** 0.5
        return {'x': jax.random.normal(ks[0], (BATCH, SEQ_LEN, D_MODEL), dtype=jnp.float32), 'Wq': jax.random.normal(ks[1], (D_MODEL, D_MODEL), dtype=jnp.float32) * std, 'Wk': jax.random.normal(ks[2], (D_MODEL, D_MODEL), dtype=jnp.float32) * std, 'Wv': jax.random.normal(ks[3], (D_MODEL, D_MODEL), dtype=jnp.float32) * std, 'Wo': jax.random.normal(ks[4], (D_MODEL, D_MODEL), dtype=jnp.float32) * std}
    _L0_attn_in = _L0_attn_setup()

    def _L0_ffn_setup():
        import jax, jax.numpy as jnp
        import numpy as np
        EPS = 1e-06
        Q_B = 128.0

        def layer_norm(x):
            mean = jnp.mean(x, axis=-1, keepdims=True)
            var = jnp.var(x, axis=-1, keepdims=True)
            return (x - mean) / jnp.sqrt(var + EPS)

        def absmax_quant(x):
            gamma = jnp.max(jnp.abs(x), axis=-1, keepdims=True)
            x_hat = jnp.clip(x * Q_B / gamma, -Q_B + EPS, Q_B - EPS)
            return x_hat * gamma / Q_B

        def ternarize_weights(w):
            gamma = jnp.mean(jnp.abs(w))
            return jnp.sign(jnp.round(w / (gamma + EPS))) * gamma

        def bitlinear(x, w):
            xn = layer_norm(x)
            x_hat = xn + jax.lax.stop_gradient(absmax_quant(xn) - xn)
            w_hat = w + jax.lax.stop_gradient(ternarize_weights(w) - w)
            return jnp.einsum('bsd,od->bso', x_hat, w_hat)
        key = jax.random.key(seed)
        k1, k2, k3 = jax.random.split(key, 3)
        B, S, D = (4, 512, 512)
        x = jax.random.normal(k1, (B, S, D), dtype=jnp.float32)
        w_fc = jax.random.normal(k2, (4 * D, D), dtype=jnp.float32) / np.sqrt(D)
        w_proj = jax.random.normal(k3, (D, 4 * D), dtype=jnp.float32) / np.sqrt(4 * D)
        return {'x': x, 'w_fc': w_fc, 'w_proj': w_proj}
    _L0_ffn_in = _L0_ffn_setup()
    _d = {'L0_attn_x': _L0_attn_in['x'], 'L0_attn_Wq': _L0_attn_in['Wq'], 'L0_attn_Wk': _L0_attn_in['Wk'], 'L0_attn_Wv': _L0_attn_in['Wv'], 'L0_attn_Wo': _L0_attn_in['Wo'], 'L0_ffn_w_fc': _L0_ffn_in['w_fc'], 'L0_ffn_w_proj': _L0_ffn_in['w_proj']}
    _x0 = _d['L0_attn_x']
    _d['L0_attn_x'] = jax.random.normal(jax.random.fold_in(jax.random.key(seed), 1), (8, 512, 512), dtype=_x0.dtype)
    del _x0
    return _d

def reference(L0_attn_x, L0_attn_Wq, L0_attn_Wk, L0_attn_Wv, L0_attn_Wo, L0_ffn_w_fc, L0_ffn_w_proj):

    def _L0_attn_ref(x, Wq, Wk, Wv, Wo):
        import jax, jax.numpy as jnp
        import numpy as np
        import math
        D_MODEL = 512
        NUM_HEADS = 16
        D_K = D_MODEL // NUM_HEADS
        SEQ_LEN = 512
        THETA = 10000.0
        BATCH = 2

        def _rope(t):
            S = t.shape[-2]
            dk = t.shape[-1]
            inv_freq = jnp.exp(-math.log(THETA) * jnp.arange(0, dk, 2, dtype=jnp.float32) / dk)
            pos = jnp.arange(S, dtype=jnp.float32)
            freqs = pos[:, None] * inv_freq[None, :]
            cos = jnp.cos(freqs)
            sin = jnp.sin(freqs)
            t1 = t[..., ::2]
            t2 = t[..., 1::2]
            rot = jnp.stack([t1 * cos - t2 * sin, t1 * sin + t2 * cos], axis=-1)
            return rot.reshape(t.shape)
        B, S, D = x.shape
        H, dk = (NUM_HEADS, D // NUM_HEADS)

        def split_heads(t):
            return t.reshape(B, S, H, dk).transpose(0, 2, 1, 3)
        q = split_heads(x @ Wq.T)
        k = split_heads(x @ Wk.T)
        v = split_heads(x @ Wv.T)
        q = _rope(q)
        k = _rope(k)
        scores = jnp.einsum('bhqd,bhkd->bhqk', q, k) / math.sqrt(dk)
        causal = jnp.tril(jnp.ones((S, S), dtype=bool))
        scores = jnp.where(causal[None, None], scores, -jnp.inf)
        attn = jax.nn.softmax(scores, axis=-1)
        ctx = jnp.einsum('bhqk,bhkd->bhqd', attn, v)
        ctx = ctx.transpose(0, 2, 1, 3).reshape(B, S, D)
        return ctx @ Wo.T

    def _L0_ffn_ref(x, w_fc, w_proj):
        import jax, jax.numpy as jnp
        import numpy as np
        EPS = 1e-06
        Q_B = 128.0

        def layer_norm(x):
            mean = jnp.mean(x, axis=-1, keepdims=True)
            var = jnp.var(x, axis=-1, keepdims=True)
            return (x - mean) / jnp.sqrt(var + EPS)

        def absmax_quant(x):
            gamma = jnp.max(jnp.abs(x), axis=-1, keepdims=True)
            x_hat = jnp.clip(x * Q_B / gamma, -Q_B + EPS, Q_B - EPS)
            return x_hat * gamma / Q_B

        def ternarize_weights(w):
            gamma = jnp.mean(jnp.abs(w))
            return jnp.sign(jnp.round(w / (gamma + EPS))) * gamma

        def bitlinear(x, w):
            xn = layer_norm(x)
            x_hat = xn + jax.lax.stop_gradient(absmax_quant(xn) - xn)
            w_hat = w + jax.lax.stop_gradient(ternarize_weights(w) - w)
            return jnp.einsum('bsd,od->bso', x_hat, w_hat)
        h = bitlinear(x, w_fc)
        h = jax.nn.gelu(h, approximate=False)
        return bitlinear(h, w_proj)
    x = L0_attn_x
    xn = _layernorm(x, axis=-1)
    s = _L0_attn_ref(xn, L0_attn_Wq, L0_attn_Wk, L0_attn_Wv, L0_attn_Wo)
    g = _silu(_L0_ffn_ref(xn, L0_ffn_w_fc, L0_ffn_w_proj))
    x = x + s * g
    return x

_drawn_inputs = setup_inputs


def setup_inputs(seed=0):
    import zlib

    import numpy as np

    out = dict(_drawn_inputs(seed))
    spreads = {}
    factors = {}
    for name, (base, spread) in spreads.items():
        noise = np.random.default_rng([zlib.crc32(name.encode()), seed]).standard_normal(out[name].shape)
        drawn = base * np.exp(spread * noise) if base else spread * noise
        out[name] = jnp.asarray(drawn.astype(out[name].dtype))
    for name, factor in factors.items():
        out[name] = (out[name] * factor).astype(out[name].dtype)
    return out
```

```python
from contextlib import ExitStack

import concourse.bass as bass
from concourse import mybir

F32 = mybir.dt.float32
F16 = mybir.dt.float16
BF16 = mybir.dt.bfloat16
ALU = mybir.AluOpType
ACT = mybir.ActivationFunctionType
AX_X = mybir.AxisListType.X
RMAX = bass.bass_isa.ReduceOp.max
RADD = bass.bass_isa.ReduceOp.add

P = 128
NB, S, D = 8, 512, 512
H, DK = 16, 32
NF = DK // 2
F = 4 * D
NT = S // P
ND = D // P
FC = F // P
HS = P // NF
GH = P // DK
NG = H // GH
KS = 3 * DK
KM = KS + 2
ROPE_SHRINK = 1.0 / 16
LN_EPS, BIT_EPS = 1e-5, 1e-6
MASKED = -1e30
KEY_COLS = [0, 512, 1024, 896]
PROBS = 1280
PER_ROUND = {3: 2, 2: 2, 1: 4, 0: 8}
ROUNDS = [(i, h, PER_ROUND[i]) for i in (3, 2, 1, 0) for h in range(0, H, PER_ROUND[i])]
NR = len(ROUNDS)
DOWN_MATMULS = 2 * FC
DOWN_BESIDE_SCORES = (NT - 1) * DOWN_MATMULS - 8
DOWN_BESIDE_EXP = 12
X_BANKS = (3, 4, 5, 2)


def program(nc, x, w_q, w_k, w_v, w_o, w_fc, w_proj, rope_cos, rope_sin, out):
    with ExitStack() as ctx:
        def sb(name, shape, dt):
            return ctx.enter_context(nc.sbuf_tensor(name, shape, dt))

        def sem(name):
            return ctx.enter_context(nc.semaphore(name))

        qkT = sb("qkT", [P, 2, 2, ND, 2, 2, P], F16)
        voT = sb("voT", [P, 2, 2, ND, D], F16)
        fcT = sb("fcT", [P, ND, F], F16)
        projT = sb("projT", [P, FC, D], F16)
        stacks = sb("stacks", [P, 2, H, S], F16)
        q_stack, k_stack = stacks[:, 0], stacks[:, 1]
        arena = sb("arena", [P, 2, GH, PROBS], F32)
        probs = arena[:]
        arena_f = arena[:].rearrange("p a b c -> p (a b c)")
        hid = arena_f[:, 0:8192].bitcast(F16).rearrange("p (s f t) -> p s f t", s=2, f=FC)
        rope_prods = arena_f[:, 8192:10240].rearrange("p (k t) -> p k t", k=4)
        result = rope_prods
        xr_buf = sb("xr_buf", [P, NT, D], F32)
        x_sb = xr_buf[:]
        rope_sum = xr_buf[:].rearrange("p (a b) t -> p a b t", a=2)
        xh_buf = sb("xh_buf", [P, NT, D], F32)
        xhat = xh_buf[:]
        gelu_out = xh_buf[:, 0:2, :]
        hid_f32 = xh_buf[:, 2:4, :]
        xT = sb("xT", [P, 2, ND, S], F16)
        rope_tab = sb("rope_tab", [P, 2, S], F32)
        mix = sb("mix", [P, 2, S], F32)
        rope_row = mix[:]
        tanh_sb = xr_buf[:]
        neg_max = mix[:, 0, 0:NT * H].rearrange("p (i h) -> p i h", i=NT)
        max_parts = mix[:, 0, 64:128].bitcast(F16).rearrange("p (i s h) -> p i s h", i=NT, s=2)
        bn = mix[:, 0, 128:128 + 6 * NT].rearrange("p (t k) -> p t k", t=NT)
        maxT = mix[0:2 * H, 1, 0:S // 2].bitcast(F16)
        split_buf = sb("split_buf", [P, 2, 4, S], F16)
        split_f = split_buf[:].rearrange("p a b t -> p (a b t)").bitcast(F32)
        squares = split_f[:, 0:1024].rearrange("p (a t) -> p a t", a=2)
        ctx_f32 = split_f[:, 0:1024].rearrange("p (a t) -> p a t", a=2)
        inv_sums = split_f[:, 1024:1536]
        sq_sum = split_f[:, 1536:2048]
        c_diag = split_f[:, 1536:2048].rearrange("p (t n) -> p t n", t=NT)
        first_c_diag = mix[:, 1, :].rearrange("p (t n) -> p t n", t=NT)
        v_sb = sb("v_sb", [P, NT, D], F32)
        ctxT = sb("ctxT", [P, 2, NG, S], F16)
        gate = sb("gate", [P, NT, D], F32)
        resid = sb("resid", [P, 2, D], F32)
        w_rowsum = sb("w_rowsum", [P, D], F16)
        ident16 = sb("ident16", [P, P], F16)
        ident_bf = sb("ident_bf", [P, P], BF16)
        ident32 = sb("ident32", [P, P], F32)
        mask_q = sb("mask_q", [P, P], BF16)
        ones32 = sb("ones32", [P, P], F32)
        ones16 = sb("ones16", [P, P], F16)
        mean_var = sb("mean_var", [P, NT, 2], F32)
        ln = sb("ln", [P, 8, NT], F32)
        norm_c = sb("norm_c", [P, NT], F32)
        minus_half = sb("minus_half", [P, NT], F32)
        ffn = sb("ffn", [P, 12, NT], F32)
        gate_scale = sb("gate_scale", [P, 2, NT], F32)
        w_part = ffn[:].rearrange("p k t -> p (k t)")[:, 0:8]
        w_all = sb("w_all", [P, 6], F32)
        scl = sb("scl", [P, 20], F32)

        raw_attn = [gate[:], ctxT[:].rearrange("p a b t -> p (a b t)").bitcast(F32).rearrange("p (a t) -> p a t", a=ND),
                    v_sb[:], rope_prods]
        raw_fc = arena_f[:, 0:8192].rearrange("p (c d) -> p c d", c=FC)
        raw_proj = stacks[:].rearrange("p a h t -> p (a h t)").bitcast(F32).rearrange("p (c d) -> p c d", c=ND)
        ring = split_buf[:]
        ring = ring.rearrange("p a (b s) t -> p (a b) s t", s=2)
        below = gate[:].rearrange("p a t -> p (a t)").bitcast(F16).rearrange("p (a t) -> p a t", a=8)
        magnitudes = ctxT[:].rearrange("p a b t -> p (a b t)").bitcast(F32)

        banks = ctx.enter_context(nc.psum_tensor("banks", [P, 8, 512], F32))
        banks16 = banks[:].rearrange("p b c -> p (b c)").bitcast(F16).rearrange("p (b c) -> p b c", b=8)
        TURN_BANKS = (6, 7, 0, 1)
        st_region = [banks[:, 0:3, :].rearrange("p b c -> p (b c)"), banks[:, 3:6, :].rearrange("p b c -> p (b c)")]

        w_dma = [sem(f"w_dma{i}") for i in range(6)]
        tab_dma, ones_dma = sem("tab_dma"), sem("ones_dma")
        stood_alone = sem("stood_alone")
        consts = sem("consts")
        w_max_ready, w_max_all = sem("w_max_ready"), sem("w_max_all")
        w_abs_part, w_abs_ready, w_abs_all = sem("w_abs_part"), sem("w_abs_ready"), sem("w_abs_all")
        attn_scl_step, ffn_scl_step = sem("attn_scl_step"), sem("ffn_scl_step")
        w_hi_ready, w_unit_ready = sem("w_hi_ready"), sem("w_unit_ready")
        w_below_pool, w_below_dve = sem("w_below_pool"), sem("w_below_dve")
        w_turned, w_kept = sem("w_turned"), sem("w_kept")
        thresholds = sem("thresholds")
        rowsum_ps, rowsum_kept = sem("rowsum_ps"), sem("rowsum_kept")
        x_dma, out_dma, max_dma = sem("x_dma"), sem("out_dma"), sem("max_dma")
        resid_dma = [sem("resid_dma0"), sem("resid_dma1")]
        stack_dma = [sem("stack_dma0"), sem("stack_dma1")]
        bn_ready, mv_ready, ln_step = sem("bn_ready"), sem("mv_ready"), sem("ln_step")
        xhat_ready, diag_ready = sem("xhat_ready"), sem("diag_ready")
        xT_ps, xhi_ready, xlo_ready = sem("xT_ps"), sem("xhi_ready"), sem("xlo_ready")
        c_ps, rope_row_ready = sem("c_ps"), sem("rope_row_ready")
        qk_ps, rope_prod_ready, rope_sum_ready = sem("qk_ps"), sem("rope_prod_ready"), sem("rope_sum_ready")
        rot_hi_ready, rot_lo_ready = sem("rot_hi_ready"), sem("rot_lo_ready")
        v_ps, v_ready = sem("v_ps"), sem("v_ready")
        wo_ps, scaled_ready, result_ready = sem("wo_ps"), sem("scaled_ready"), sem("result_ready")
        fc_ps, gelu_ready, hid_ready = sem("fc_ps"), sem("gelu_ready"), sem("hid_ready")
        hid_hi_ready, hid_lo_ready = sem("hid_hi_ready"), sem("hid_lo_ready")
        sq_ready, sq_added, sq_ps = sem("sq_ready"), sem("sq_added"), sem("sq_ps")
        down_ps, down_kept = sem("down_ps"), sem("down_kept")
        s_ps, max_ready, max_hi, max_lo = sem("s_ps"), sem("max_ready"), sem("max_hi"), sem("max_lo")
        maxT_ps, maxT_ready = sem("maxT_ps"), sem("maxT_ready")
        sums_read, ffn_step, var_ready, rstd_ready = sem("sums_read"), sem("ffn_step"), sem("var_ready"), sem("rstd_ready")
        ln_ready = sem("ln_ready")
        centred, tanh_ready, gate_ready = sem("centred"), sem("tanh_ready"), sem("gate_ready")
        st_ps, probs_ready, probs_masked, pv_ps = sem("st_ps"), sem("probs_ready"), sem("probs_masked"), sem("pv_ps")
        pv_kept, inv_ready, ctx_ready = sem("pv_kept"), sem("inv_ready"), sem("ctx_ready")
        ctx_hi, ctx_lo = sem("ctx_hi"), sem("ctx_lo")

        S_Q, S_K, S_V, S_O, INV, EXP_SCALE, SVO = 0, 1, 2, 3, 4, 8, 9
        G_FC, G_PROJ, INV_G, THR, MTHR, BIT_EPS_G, HALF_GP = 10, 11, 12, 13, 15, 17, 18

        def col(c):
            return scl[:, c:c + 1]

        units = [("attn", m, o) for m in range(3) for o in range(ND)]
        n_first = len(units)
        units += [("fc", o) for o in range(0, FC, 2)]
        units += [("proj", o, f) for o in range(ND) for f in range(0, 4, 2)]
        n_tern = len(units) - n_first
        units += [("attn", 3, o) for o in range(ND)]
        n_units = len(units)

        def raw_parts(unit):
            if unit[0] == "fc":
                return [raw_fc[:, unit[1] + k, :] for k in range(2)]
            return [raw_proj[:, unit[1], (unit[2] + k) * 512:(unit[2] + k + 1) * 512] for k in range(2)]

        block = ctx.enter_context(nc.Block())

        def alone(eng):
            eng.sem_inc(stood_alone, 1)

        @block.sync
        def _(sp):
            def load_weight(raw, w, n):
                sp.dma_start(raw, w.rearrange("(c p) d -> p c d", p=P)).then_inc(w_dma[n], 16)

            for m, w in enumerate((w_q, w_k, w_v)):
                load_weight(raw_attn[m], w, m)
            sp.dma_start(x_sb, x[0].rearrange("(t p) d -> p t d", p=P)).then_inc(x_dma, 16)
            sp.dma_start(rope_tab[:, 0, :], rope_cos).then_inc(tab_dma, 16)
            sp.dma_start(rope_tab[:, 1, :], rope_sin).then_inc(tab_dma, 16)
            load_weight(raw_fc, w_fc, 4)
            load_weight(raw_proj, w_proj, 5)
            load_weight(raw_attn[3], w_o, 3)

            def load_resid(b, t):
                if t >= 2:
                    sp.wait_ge(result_ready, b * NT + t - 1)
                sp.dma_start(resid[:, t % 2, :], x[b].rearrange("(t p) d -> t p d", p=P)[t]).then_inc(resid_dma[t % 2], 16)

            def store_result(b):
                for t in range(NT):
                    sp.wait_ge(result_ready, b * NT + t + 1)
                    sp.dma_start(out[b].rearrange("(t p) d -> t p d", p=P)[t], result[:, t, :]).then_inc(out_dma, 16)
                    if t + 2 < NT:
                        load_resid(b, t + 2)

            def body(b, first=False, last=False):
                if not first:
                    load_resid(b - 1, 0)
                    load_resid(b - 1, 1)
                else:
                    sp.wait_ge(w_kept, n_units)
                    sp.dma_start(k_stack[KS:KM, :, :], ones16[:]).then_inc(ones_dma, 16)
                for pair in range(4):
                    stack, heads = (q_stack, k_stack)[pair // 2], slice(HS * (pair % 2), HS * (pair % 2 + 1))
                    if pair == 0 and not first:
                        sp.wait_ge(st_ps, b * H)
                    sp.wait_ge(rot_lo_ready, b * 8 + 2 * pair + 2)
                    order = ((0, 0, 1), (0, 1, 0))[pair // 2]
                    for third, part in enumerate(order):
                        for half in range(2):
                            row = third * DK + half * NF
                            sp.dma_start(stack[row:row + NF, heads, :], split_buf[:, pair % 2, 2 * part + half, :]
                                         ).then_inc(stack_dma[pair % 2], 16)
                if not last:
                    sp.dma_start(x_sb, x[b + 1].rearrange("(t p) d -> p t d", p=P)).then_inc(x_dma, 16)
                if not first:
                    store_result(b - 1)
                sp.wait_ge(maxT_ready, b + 1)
                sp.dma_start(q_stack[KS:KM, :, :], maxT[:, :]).then_inc(max_dma, 16)

            body(0, first=True)
            with sp.Fori(1, NB - 1) as b:
                body(b)
            body(NB - 1, last=True)
            load_resid(NB - 1, 0)
            load_resid(NB - 1, 1)
            store_result(NB - 1)
            sp.wait_ge(out_dma, NB * NT * 16)

        @block.tensor
        def _(pe):
            pe.wait_ge(consts, 1)

            def turn_weights(first, end):
                for u in range(first, end):
                    pe.wait_ge(w_unit_ready, u + 1)
                    if u >= 4:
                        pe.wait_ge(w_kept, u - 3)
                    for k in range(8):
                        mm = pe.transpose(banks16[:, TURN_BANKS[u % 4], k * P:(k + 1) * P],
                                          ring[:, u % 4, k // 4, (k % 4) * P:(k % 4 + 1) * P], ident16[:])
                    mm.then_inc(w_turned, 1)

            def ternary_row_sums():
                pe.wait_ge(w_kept, n_units)
                for f in range(FC):
                    mm = pe.matmul(banks[:, 6, :], ones16[:], projT[:, f, :], start=(f == 0), stop=(f == FC - 1))
                mm.then_inc(rowsum_ps, 1)

            def three_products(out_ap, hi_lo, n, key):
                for c in range(n):
                    for k, (a, r) in enumerate(((0, 0), (0, 1), (1, 0))):
                        lhs, rhs = hi_lo(a, r, c)
                        mm = pe.matmul(out_ap, lhs, rhs, start=(c == 0 and k == 0), stop=(c == n - 1 and k == 2))
                return mm

            def out_projection(b):
                for t in range(NT):
                    if t == 0:
                        pe.wait_ge(ctx_lo, b * NG + NG)
                    if t >= 2:
                        pe.wait_ge(scaled_ready, b * NT + t - 1)
                    three_products(banks[:, 6 + t % 2, :],
                                   lambda a, r, c: (ctxT[:, a, c, t * P:(t + 1) * P], voT[:, 1, r, c, :]),
                                   NG, "o").then_inc(wo_ps, 1)

            def turn_tokens(b, t, first=False):
                if t == 0 and not first:
                    pe.wait_ge(probs_ready, b * H - 1)
                if t == 3 and not first:
                    pe.wait_ge(probs_ready, b * H)
                pe.wait_ge(xhat_ready, b * NT + t + 1)
                for c in range(ND):
                    mm = pe.transpose(banks[:, X_BANKS[t], c * P:(c + 1) * P], xhat[:, t, c * P:(c + 1) * P], ident32[:])
                mm.then_inc(xT_ps, 1)

            def spread_norms(b, first=False):
                if first:
                    pe.wait_ge(w_kept, n_first)
                pe.wait_ge(diag_ready, b * NT + NT)
                for t in range(NT):
                    mm = pe.matmul(banks[:, 1, t * P:(t + 1) * P], ones32[:],
                                   (first_c_diag if first else c_diag)[:, t, :], start=True, stop=True)
                mm.then_inc(c_ps, 1)

            def body(b, first=False, last=False):
                for t in range(NT):
                    pe.wait_ge(xlo_ready, b * NT + t + 1)
                    if t == 1:
                        pe.wait_ge(rope_row_ready, b * 2 + 2)
                    if t >= 2:
                        pe.wait_ge(v_ready, b * NT + t - 1)
                    three_products(banks[:, t % 2, :],
                                   lambda a, r, c: (xT[:, a, c, t * P:(t + 1) * P], voT[:, 0, r, c, :]),
                                   ND, "v").then_inc(v_ps, 1)
                for pair in range(4):
                    if pair == 2 and first:
                        pe.wait_ge(v_ready, NT)
                        turn_weights(n_first, n_units)
                        ternary_row_sums()
                    if pair >= 2:
                        pe.wait_ge(rope_prod_ready, b * 16 + 4 * (pair - 2) + 4)
                    for half in range(2):
                        three_products(banks[:, 2 + 2 * (pair % 2) + half, :],
                                       lambda a, r, c: (qkT[:, pair // 2, r, c, pair % 2, half, :], xT[:, a, c, :]),
                                       ND, "qk").then_inc(qk_ps, 1)
                if not first:
                    out_projection(b - 1)
                for f in range(FC):
                    if f < 2:
                        pe.wait_ge(v_ready, b * NT + 3 + f)
                    else:
                        pe.wait_ge(gelu_ready, b * FC + f - 1)
                    for c in range(ND):
                        for part in range(2):
                            mm = pe.matmul(banks[:, f % 2, :], fcT[:, c, f * P:(f + 1) * P], xT[:, part, c, :],
                                           start=(c == 0 and part == 0), stop=(c == ND - 1 and part == 1))
                    mm.then_inc(fc_ps, 1)

                def down():
                    for t in range(NT):
                        if t == 0:
                            if first:
                                pe.wait_ge(rowsum_kept, 1)
                            else:
                                pe.wait_ge(scaled_ready, b * NT)
                            pe.wait_ge(gelu_ready, b * FC + FC)
                        if t >= 2:
                            pe.wait_ge(down_kept, b * 2 + t - 1)
                        order = [(f, part) for f in range(FC) for part in range(2)]
                        if t == NT - 1:
                            order = [(f, part) for part in range(2) for f in range(FC)]
                        for f, part in order:
                            if t == 0 and part == 0:
                                pe.wait_ge(hid_lo_ready, b * FC + f + 1)
                            lhs = hid[:, part, f, t * P:(t + 1) * P]
                            ends = dict(start=(f == 0 and part == 0), stop=(f == FC - 1 and part == 1))
                            if t < NT - 1:
                                pe.matmul(banks[:, 0, t:t + 1], lhs, ones16[:, 0:1], **ends)
                            mm = pe.matmul(banks[:, 6 + t % 2, :], lhs, projT[:, f, :], **ends)
                            if ends["stop"]:
                                mm.then_inc(down_ps, 1)
                            yield

                downs = down()
                given = 0
                for r, (i, h0, n) in enumerate(ROUNDS):
                    if r == 0:
                        for s in stack_dma:
                            pe.wait_ge(s, (b + 1) * 192)
                        pe.wait_ge(rope_prod_ready, b * 16 + 16)
                    if r >= 2:
                        pe.wait_ge(max_ready, b * NR + r - 1)
                    keys = (i + 1) * P
                    per_bank = 512 // keys
                    for k in range(n):
                        bank, at = 2 + 2 * (r % 2) + k // per_bank, (k % per_bank) * keys
                        pe.matmul(banks[:, bank, at:at + keys], q_stack[0:KS, h0 + k, i * P:(i + 1) * P],
                                  k_stack[0:KS, h0 + k, 0:keys], start=True, stop=False)
                        mm = pe.matmul(banks[:, bank, at + i * P:at + keys], ident_bf[:], mask_q[:], start=False, stop=True)
                    mm.then_inc(s_ps, 1)
                    while given < DOWN_BESIDE_SCORES * (r + 1) // NR:
                        next(downs)
                        given += 1
                pe.wait_ge(max_lo, b + 1)
                for i in range(NT):
                    mm = pe.transpose(banks16[0:2 * H, 1, i * P:(i + 1) * P],
                                      max_parts[:, i].rearrange("p s h -> p (s h)"), ident16[:])
                mm.then_inc(maxT_ps, 1)
                while given < (NT - 1) * DOWN_MATMULS:
                    next(downs)
                    given += 1
                for f in range(FC):
                    for part in range(2):
                        pe.matmul(banks[:, 0, NT - 1:NT], hid[:, part, f, S - P:S], ones16[:, 0:1],
                                  start=(f == 0 and part == 0), stop=(f == FC - 1 and part == 1))
                pe.wait_ge(sq_added, b * (FC - 1) + FC - 1)
                for t in range(NT):
                    mm = pe.matmul(banks[:, 0, NT + t:NT + t + 1], sq_sum[:, t * P:(t + 1) * P], ones32[:, 0:1], start=True, stop=True)
                mm.then_inc(sq_ps, 1)
                while given < NT * DOWN_MATMULS - DOWN_BESIDE_EXP:
                    next(downs)
                    given += 1

                def scores(h):
                    if h == 0 and first:
                        pe.wait_ge(ones_dma, 16)
                    if h == 0:
                        pe.wait_ge(max_dma, (b + 1) * 16)
                    if h == 1:
                        pe.wait_ge(sums_read, b + 1)
                    if h >= 2:
                        pe.wait_ge(probs_ready, b * H + h - 1)
                    ps = st_region[(h + 1) % 2]
                    for j in (0, 1, 3, 2):
                        at, n = KEY_COLS[j], S - j * P
                        mm = pe.matmul(ps[:, at:at + n], k_stack[0:KM, h, j * P:(j + 1) * P], q_stack[0:KM, h, j * P:S],
                                       start=True, stop=True)
                    mm.then_inc(st_ps, 1)

                def weigh(g, j):
                    if j == 0:
                        pe.wait_ge(probs_masked, b * H + GH * (g + 1))
                        if g == 0:
                            pe.wait_ge(centred, b * NT + NT)
                        else:
                            pe.wait_ge(pv_kept, (b * NG + g) * 2)
                    at, n = KEY_COLS[j], S - j * P
                    for bank in (6, 7):
                        for k in range(GH):
                            head = GH * g + k
                            lhs = v_sb[:, j, head * DK:(head + 1) * DK] if bank == 6 else ones32[:, 0:DK]
                            mm = pe.matmul(banks[k * DK:(k + 1) * DK, bank, j * P:S], lhs, probs[:, g % 2, k, at:at + n],
                                           start=(j == 0), stop=(j == NT - 1), tile_position=(0, k * DK))
                    if j == NT - 1:
                        mm.then_inc(pv_ps, 1)

                for g in range(NG + 1):
                    for k in range(GH):
                        if g < NG:
                            scores(GH * g + k)
                        for _ in range(DOWN_BESIDE_EXP // (GH - 1) if g == 0 and k < GH - 1 else 0):
                            next(downs)
                        if g > 0 and k > 0:
                            weigh(g - 1, k - 1)
                        if g == NG and not last:
                            if k == 0:
                                for t in range(3):
                                    turn_tokens(b + 1, t)
                            if k == 1:
                                turn_tokens(b + 1, 3)
                                spread_norms(b + 1)
                    if g > 0:
                        weigh(g - 1, NT - 1)

            turn_weights(0, n_first)
            for t in range(NT):
                turn_tokens(0, t, first=True)
            spread_norms(0, first=True)
            body(0, first=True)
            with pe.Fori(1, NB - 1) as b:
                body(b)
            body(NB - 1, last=True)
            out_projection(NB - 1)

        @block.scalar
        def _(act):
            def keep_weights(u):
                unit = units[u]
                act.wait_ge(w_turned, u + 1)
                src = banks16[:, TURN_BANKS[u % 4], :]
                if unit[0] == "fc":
                    dst = fcT[:, :, unit[1] * P:(unit[1] + 2) * P].rearrange("p c (o n) -> p o c n", o=2)
                    mm = nc.scalar.copy(dst, src.rearrange("p (o c n) -> p o c n", o=2, c=ND))
                elif unit[0] == "proj":
                    _, o, f = unit
                    mm = nc.scalar.copy(projT[:, 4 * f:4 * f + 8, o * P:(o + 1) * P], src.rearrange("p (f n) -> p f n", f=8))
                else:
                    _, m, o = unit
                    src = src.rearrange("p (s c n) -> p s c n", s=2, c=ND)
                    if m >= 2:
                        mm = nc.scalar.copy(voT[:, m - 2, :, :, o * P:(o + 1) * P], src)
                    for part, half in [(p, h) for p in range(2) for h in range(2)] if m < 2 else []:
                        part_src = src[:, part].rearrange("p c (h f two) -> p c f h two", h=GH, two=2)[:, :, :, :, half]
                        dst = qkT[:, m, part, :, o // 2, half, :].rearrange("p c (f h) -> p c f h", h=HS)
                        mm = nc.scalar.copy(dst[:, :, :, GH * (o % 2):GH * (o % 2) + GH], part_src)
                mm.then_inc(w_kept, 1)

            def sum_magnitudes(m, k):
                raw = (raw_fc, raw_proj)[m].rearrange("p c d -> p (c d)")
                act.wait_ge(w_dma[4 + m], 16)
                if m or k:
                    act.wait_ge(w_abs_part, 4 * m + k)
                nc.scalar.activation(magnitudes, raw[:, k * 2048:(k + 1) * 2048], ACT.Abs,
                                     accum_out=w_part[:, 4 * m + k:4 * m + k + 1]).then_inc(w_abs_part, 1)

            def normalise(b, t):
                act.wait_ge(ln_ready, b + 1)
                nc.scalar.activation(xhat[:, t, :], x_sb[:, t, :], ACT.Identity, scale=ln[:, 6, t:t + 1],
                                     bias=ln[:, 7, t:t + 1]).then_inc(xhat_ready, 1)

            def split_tokens(b):
                for t in range(NT):
                    act.wait_ge(xT_ps, b * NT + t + 1)
                    nc.scalar.copy(xT[:, 0, :, t * P:(t + 1) * P],
                                   banks[:, X_BANKS[t], :].rearrange("p (c n) -> p c n", c=ND)).then_inc(xhi_ready, 1)

            for u in range(n_first):
                keep_weights(u)
                if u == 7:
                    for t in range(NT):
                        normalise(0, t)
            split_tokens(0)

            def body(b, first=False, last=False):
                for t in range(NT):
                    if first:
                        sum_magnitudes(0, t)
                    act.wait_ge(v_ps, b * NT + t + 1)
                    nc.scalar.activation(v_sb[:, t, :], banks[:, t % 2, :], ACT.Copy, scale=norm_c[:, t:t + 1]).then_inc(v_ready, 1)

                if first:
                    for k in range(4):
                        sum_magnitudes(1, k)
                    for u in range(n_first, n_units):
                        keep_weights(u)
                    act.wait_ge(rowsum_ps, 1)
                    nc.scalar.copy(w_rowsum[:], banks[:, 6, :]).then_inc(rowsum_kept, 1)
                for pair in range(4):
                    for half in range(2):
                        act.wait_ge(rope_sum_ready, b * 8 + 2 * pair + half + 1)
                        if half == 0 and pair >= 2:
                            act.wait_ge(stack_dma[pair % 2], b * 192 + 96)
                        if half == 0 and pair == 0 and not first:
                            act.wait_ge(ctx_lo, b * NG)
                        nc.scalar.copy(split_buf[:, pair % 2, half, :], rope_sum[:, pair % 2, half, :]).then_inc(rot_hi_ready, 1)
                def square(f):
                    act.wait_ge(hid_ready, b * FC + f + 1)
                    if f == 0:
                        for s in stack_dma:
                            act.wait_ge(s, (b + 1) * 192)
                    if f >= 3:
                        act.wait_ge(sq_added, b * (FC - 1) + f - 2)
                    dst = sq_sum[:] if f == 0 else squares[:, f % 2, :]
                    nc.scalar.activation(dst, hid_f32[:, f % 2, :], ACT.Square).then_inc(sq_ready, 1)

                for f in range(FC):
                    act.wait_ge(fc_ps, b * FC + f + 1)
                    if f >= 2:
                        act.wait_ge(hid_ready, b * FC + f - 1)
                    nc.scalar.activation(gelu_out[:, f % 2, :], banks[:, f % 2, :], ACT.Gelu, scale=col(G_FC)).then_inc(gelu_ready, 1)
                    if f >= 1:
                        square(f - 1)
                square(FC - 1)
                for t in range(2):
                    act.wait_ge(down_ps, b * NT + t + 1)
                    nc.scalar.copy(gate[:, t, :], banks[:, 6 + t % 2, :]).then_inc(down_kept, 1)

                for h in range(H):
                    g = h // GH
                    act.wait_ge(st_ps, b * H + h + 1)
                    if h % GH == 0 and g == 1 and not first:
                        act.wait_ge(out_dma, b * NT * 16)
                    if h % GH == 0 and g >= 2:
                        act.wait_ge(pv_ps, b * NG + g - 1)
                    nc.scalar.activation(probs[:, g % 2, h % GH, :], st_region[(h + 1) % 2][:, 0:PROBS], ACT.Exp,
                                         scale=col(EXP_SCALE)).then_inc(probs_ready, 1)
                    if not last and h in (5, 7, 9, 11):
                        normalise(b + 1, (h - 5) // 2)
                if not last:
                    split_tokens(b + 1)
                for t in range(NT):
                    act.wait_ge(centred, b * NT + NT)
                    nc.scalar.activation(tanh_sb[:, t, :], gate[:, t, :], ACT.Tanh,
                                         scale=gate_scale[:, 0, t:t + 1]).then_inc(tanh_ready, 1)

            body(0, first=True)
            with act.Fori(1, NB - 1) as b:
                body(b)
            body(NB - 1, last=True)

        @block.vector
        def _(dve):
            def largest(m):
                dve.wait_ge(w_dma[m], 16)
                nc.vector.tensor_reduce(w_all[:, m:m + 1], raw_attn[m].rearrange("p c d -> p (c d)"), AX_X, ALU.max,
                                        apply_absolute_value=True).then_inc(w_max_ready, 1)

            def attn_step(k, ins):
                ins.then_inc(attn_scl_step, 1)
                dve.wait_ge(attn_scl_step, k)

            def split_weights(u):
                _, m, o = units[u]
                if u >= 4:
                    dve.wait_ge(w_turned, u - 3)
                nc.vector.tensor_scalar(ring[:, u % 4, 0, :], raw_attn[m][:, o, :], col(INV + m), None, ALU.mult).then_inc(w_hi_ready, 1)
                dve.wait_ge(w_hi_ready, u + 1 if u < n_first else u + 1 - n_tern)
                nc.vector.scalar_tensor_tensor(ring[:, u % 4, 1, :], raw_attn[m][:, o, :], col(INV + m), ring[:, u % 4, 0, :],
                                               ALU.mult, ALU.subtract).then_inc(w_unit_ready, 1)

            def ffn_scales(m):
                def step(k, ins):
                    ins.then_inc(ffn_scl_step, 1)
                    dve.wait_ge(ffn_scl_step, 4 * m + k)

                dve.wait_ge(w_abs_part, 4 * m + 4)
                nc.vector.tensor_reduce(w_all[:, 4 + m:5 + m], w_part[:, 4 * m:4 * m + 4], AX_X, ALU.add).then_inc(w_abs_ready, 1)
                dve.wait_ge(w_abs_all, m + 1)
                gamma = col(G_FC + m)
                step(1, nc.vector.tensor_scalar(gamma, gamma, 1.0 / (F * D), None, ALU.mult))
                step(2, nc.vector.tensor_scalar(col(THR + m), gamma, BIT_EPS, 0.5, ALU.add, ALU.mult))
                if m == 0:
                    step(3, nc.vector.reciprocal(col(INV_G), gamma))
                    step(4, nc.vector.scalar_tensor_tensor(col(BIT_EPS_G), col(INV_G), BIT_EPS, col(INV_G), ALU.mult, ALU.mult))
                else:
                    step(3, nc.vector.tensor_scalar(col(HALF_GP), gamma, 0.5, None, ALU.mult))
                nc.vector.tensor_scalar(col(MTHR + m), col(THR + m), -1.0, None, ALU.mult).then_inc(thresholds, 1)
                dve.wait_ge(thresholds, m + 1)

            def ternary(u):
                k, m, parts = u - n_first, int(units[u][0] == "proj"), raw_parts(units[u])
                nc.vector.tensor_scalar(below[:, 2 * k % 8, :], parts[0], col(MTHR + m), None, ALU.is_lt).then_inc(w_below_dve, 1)
                dve.wait_ge(w_turned, u - 3)
                dve.wait_ge(w_below_dve, k + 1)
                nc.vector.scalar_tensor_tensor(ring[:, u % 4, 0, :], parts[0], col(THR + m), below[:, 2 * k % 8, :],
                                               ALU.is_gt, ALU.subtract)
                dve.wait_ge(w_below_pool, k + 1)
                nc.vector.scalar_tensor_tensor(ring[:, u % 4, 1, :], parts[1], col(THR + m), below[:, (2 * k + 1) % 8, :],
                                               ALU.is_gt, ALU.subtract).then_inc(w_unit_ready, 1)

            def remaining_weights():
                ffn_scales(0)
                for u in range(n_first, n_first + FC // 2):
                    ternary(u)
                ffn_scales(1)
                for u in range(n_first + FC // 2, n_first + n_tern):
                    ternary(u)
                largest(3)
                dve.wait_ge(w_max_all, 2)
                attn_step(4, nc.vector.tensor_scalar(col(S_O), col(S_O), 1e-30, None, ALU.max))
                nc.vector.tensor_tensor(col(SVO), col(S_V), col(S_O), ALU.mult).then_inc(attn_scl_step, 1)
                attn_step(6, nc.vector.reciprocal(col(INV + 3), col(S_O)))
                for u in range(n_first + n_tern, n_units):
                    split_weights(u)

            for m in range(3):
                largest(m)
            dve.wait_ge(w_max_all, 1)
            attn_step(1, nc.vector.tensor_scalar(scl[:, S_Q:S_Q + 3], scl[:, S_Q:S_Q + 3], 1e-30, None, ALU.max))
            nc.vector.scalar_tensor_tensor(col(EXP_SCALE), col(S_Q), DK ** -0.5 / ROPE_SHRINK ** 2, col(S_K),
                                           ALU.mult, ALU.mult).then_inc(attn_scl_step, 1)
            attn_step(3, nc.vector.reciprocal(scl[:, INV:INV + 3], scl[:, S_Q:S_Q + 3]))

            def statistics(b):
                dve.wait_ge(x_dma, b * 16 + 16)
                for t in range(NT):
                    nc.vector.bn_stats(bn[:, t, :], x_sb[:, t, :]).then_inc(bn_ready, 1)
                dve.wait_ge(bn_ready, b * NT + NT)
                alone(dve)
                for t in range(NT):
                    nc.vector.bn_aggr(mean_var[:, t, :], bn[:, t, :]).then_inc(mv_ready, 1)

            def finish_context(b, g, count):
                dve.wait_ge(pv_kept, count * 2)
                nc.vector.reciprocal(inv_sums, inv_sums).then_inc(inv_ready, 1)
                dve.wait_ge(inv_ready, count)
                nc.vector.tensor_tensor(ctx_f32[:, g % 2, :], ctx_f32[:, g % 2, :], inv_sums, ALU.mult).then_inc(ctx_ready, 1)

            def scale_by_gate(b, sums, final=False):
                dve.wait_ge(rope_sum_ready, sums)
                if final:
                    dve.wait_ge(gate_ready, b * NT + NT)
                for t in range(NT):
                    dve.wait_ge(wo_ps, b * NT + t + 1)
                    nc.vector.scalar_tensor_tensor(result[:, t, :], banks[:, 6 + t % 2, :], gate_scale[:, 1, t:t + 1],
                                                   gate[:, t, :], ALU.mult, ALU.mult).then_inc(scaled_ready, 1)

            def split_tokens(b, first=False):
                for t in range(NT):
                    dve.wait_ge(xhi_ready, b * NT + t + 1)
                    tile = xT[:, :, :, t * P:(t + 1) * P]
                    nc.vector.tensor_tensor(tile[:, 1], banks[:, X_BANKS[t], :].rearrange("p (c n) -> p c n", c=ND), tile[:, 0],
                                            ALU.subtract).then_inc(xlo_ready, 1)
                if first:
                    dve.wait_ge(mv_ready, NT)
                    dve.wait_ge(tab_dma, 32)
                dve.wait_ge(c_ps, b + 1)
                for k in range(2):
                    nc.vector.tensor_tensor(rope_row[:, k, :], banks[:, 1, :], rope_tab[:, k, :], ALU.mult).then_inc(rope_row_ready, 1)

            def body(b, first=False, last=False):
                if first:
                    remaining_weights()
                dve.wait_ge(rope_row_ready, b * 2 + 2)
                for pair in range(4):
                    if pair == 0 and not first:
                        dve.wait_ge(gate_ready, b * NT)
                    if pair == 0 and first:
                        dve.wait_ge(w_unit_ready, n_units)
                    if pair >= 1:
                        dve.wait_ge(rope_sum_ready, b * 8 + 2 * pair)
                    dve.wait_ge(qk_ps, b * 8 + 2 * pair + 2)
                    for k, (half, table) in enumerate(((0, 0), (1, 1), (0, 1), (1, 0))):
                        nc.vector.tensor_tensor(rope_prods[:, k, :], banks[:, 2 + 2 * (pair % 2) + half, :], rope_row[:, table, :],
                                                ALU.mult).then_inc(rope_prod_ready, 1)
                    if pair >= 2:
                        dve.wait_ge(rot_lo_ready, b * 8 + 2 * (pair - 2) + 2)
                    dve.wait_ge(rope_prod_ready, b * 16 + 4 * pair + 4)
                    for half, op in enumerate((ALU.subtract, ALU.add)):
                        nc.vector.tensor_tensor(rope_sum[:, pair % 2, half, :], rope_prods[:, 2 * half, :], rope_prods[:, 2 * half + 1, :],
                                                op).then_inc(rope_sum_ready, 1)
                if not first:
                    scale_by_gate(b - 1, b * 8 + 8)
                for f in range(FC):
                    dve.wait_ge(gelu_ready, b * FC + f + 1)
                    if f >= 2:
                        dve.wait_ge(sq_ready, b * FC + f - 1)
                    nc.vector.tensor_scalar(hid_f32[:, f % 2, :], gelu_out[:, f % 2, :], col(INV_G), None, ALU.mult).then_inc(hid_ready, 1)
                    dve.wait_ge(hid_ready, b * FC + f + 1)
                    nc.vector.tensor_copy(hid[:, 0, f, :], hid_f32[:, f % 2, :]).then_inc(hid_hi_ready, 1)
                    dve.wait_ge(hid_hi_ready, b * FC + f + 1)
                    nc.vector.tensor_tensor(hid[:, 1, f, :], hid_f32[:, f % 2, :], hid[:, 0, f, :], ALU.subtract).then_inc(hid_lo_ready, 1)
                for r, (i, h0, n) in enumerate(ROUNDS):
                    if r == 0:
                        dve.wait_ge(hid_lo_ready, b * FC + FC)
                    dve.wait_ge(s_ps, b * NR + r + 1)
                    keys = (i + 1) * P
                    src = banks[:, 2 + 2 * (r % 2):4 + 2 * (r % 2), 0:512 // keys * keys]
                    if i < 2:
                        src = src.rearrange("p b (h k) -> p b h k", k=keys)
                    nc.vector.tensor_reduce(neg_max[:, i, h0:h0 + n], src, AX_X, ALU.max, negate=True).then_inc(max_ready, 1)
                dve.wait_ge(max_ready, b * NR + NR)
                nc.vector.tensor_copy(max_parts[:, :, 0, :], neg_max[:]).then_inc(max_hi, 1)
                dve.wait_ge(max_hi, b + 1)
                nc.vector.tensor_tensor(max_parts[:, :, 1, :], neg_max[:], max_parts[:, :, 0, :], ALU.subtract).then_inc(max_lo, 1)
                if not first:
                    dve.wait_ge(max_dma, b * 16)
                dve.wait_ge(maxT_ps, b + 1)
                nc.vector.tensor_copy(maxT[:, :], banks16[0:2 * H, 1, 0:S]).then_inc(maxT_ready, 1)
                if not last:
                    statistics(b + 1)
                mean, ex2 = ffn[:, 0, :], ffn[:, 1, :]
                neg_mean, msq, var, var_eps = (ffn[:, k, :] for k in range(2, 6))
                var_inv, nan_if_0, rstd, half_scale = (ffn[:, k, :] for k in range(6, 10))
                dve.wait_ge(sq_ps, b + 1)
                nc.vector.tensor_scalar(ffn[:, 0:2, :].rearrange("p k t -> p (k t)"), banks[:, 0, 0:2 * NT], 1.0 / F, None,
                                        ALU.mult).then_inc(sums_read, 1)
                dve.wait_ge(sums_read, b + 1)
                n_step = 7

                def step(k, ins):
                    ins.then_inc(ffn_step, 1)
                    dve.wait_ge(ffn_step, b * n_step + k)

                step(1, nc.vector.tensor_tensor(msq, mean, mean, ALU.mult))
                step(2, nc.vector.tensor_tensor(var, ex2, msq, ALU.subtract))
                nc.vector.tensor_scalar(var_eps, var, col(BIT_EPS_G), None, ALU.add).then_inc(var_ready, 1)
                step(3, nc.vector.tensor_scalar(neg_mean, mean, -1.0, None, ALU.mult))
                step(4, nc.vector.reciprocal(var_inv, var))
                step(5, nc.vector.tensor_tensor(nan_if_0, var, var_inv, ALU.mult))
                dve.wait_ge(rstd_ready, b + 1)
                step(6, nc.vector.scalar_tensor_tensor(gate_scale[:, 0, :], rstd, col(HALF_GP), nan_if_0, ALU.mult, ALU.mult))
                step(7, nc.vector.tensor_scalar(gate_scale[:, 1, :], gate_scale[:, 0, :], col(SVO), None, ALU.mult))
                for t in range(NT):
                    if t < 2:
                        dve.wait_ge(down_kept, b * 2 + t + 1)
                    else:
                        dve.wait_ge(down_ps, b * NT + t + 1)
                    nc.vector.scalar_tensor_tensor(gate[:, t, :], w_rowsum[:], neg_mean[:, t:t + 1],
                                                   gate[:, t, :] if t < 2 else banks[:, 6 + t % 2, :],
                                                   ALU.mult, ALU.add).then_inc(centred, 1)

                def keep_context(g):
                    if g >= 1:
                        dve.wait_ge(ctx_ready, b * NG + g)
                    if g >= 2:
                        dve.wait_ge(ctx_lo, b * NG + g - 1)
                    dve.wait_ge(pv_ps, b * NG + g + 1)
                    nc.vector.tensor_copy(ctx_f32[:, g % 2, :], banks[:, 6, :]).then_inc(pv_kept, 1)
                    nc.vector.tensor_copy(inv_sums, banks[:, 7, :]).then_inc(pv_kept, 1)

                def finish_gate(t):
                    dve.wait_ge(tanh_ready, b * NT + t + 1)
                    nc.vector.scalar_tensor_tensor(gate[:, t, :], tanh_sb[:, t, :], 1.0, gate[:, t, :],
                                                   ALU.add, ALU.mult).then_inc(gate_ready, 1)

                for g in range(NG):
                    keep_context(g)
                    if g == 2 and not last:
                        split_tokens(b + 1)
                    finish_context(b, g, b * NG + g + 1)
                for t in range(NT):
                    finish_gate(t)

            statistics(0)
            for u in range(n_first):
                split_weights(u)
            split_tokens(0, first=True)
            body(0, first=True)
            with dve.Fori(1, NB - 1) as b:
                body(b)
            body(NB - 1, last=True)
            scale_by_gate(NB - 1, NB * 8, final=True)

        @block.gpsimd
        def _(pool):
            nc.gpsimd.memset(ones32[:], 1.0)
            nc.gpsimd.memset(ones16[:], 1.0)
            nc.gpsimd.memset(ident16[:], 0.0)
            nc.gpsimd.memset(ident_bf[:], 0.0)
            nc.gpsimd.memset(ident32[:], 0.0)
            nc.gpsimd.memset(mask_q[:], 0.0)
            nc.gpsimd.memset(minus_half[:], -0.5).then_inc(ln_step, 1)
            pool.wait_ge(ln_step, 1)
            for ident in (ident16, ident_bf, ident32):
                nc.gpsimd.affine_select(ident[:], ident[:], [[-1, P]], ALU.not_equal, 1.0, base=0, channel_multiplier=1)
            nc.gpsimd.affine_select(mask_q[:], mask_q[:], [[-1, P]], ALU.is_ge, MASKED, base=0, channel_multiplier=1).then_inc(consts, 1)
            LN_STEPS = 9

            def normalise(b, first=False):
                mean, var = mean_var[:, :, 0], mean_var[:, :, 1]
                a1, r1, sq, v2, a2, r2, rr, shift = (ln[:, k, :] for k in range(8))

                def step(k, ins):
                    ins.then_inc(ln_step, 1)
                    pool.wait_ge(ln_step, b * LN_STEPS + 1 + k)
                    alone(pool)

                pool.wait_ge(mv_ready, b * NT + NT)
                if not first:
                    pool.wait_ge(v_ready, b * NT)
                    pool.wait_ge(diag_ready, b * NT)
                alone(pool)
                step(1, nc.gpsimd.tensor_scalar(a1, var, LN_EPS, None, ALU.add))
                step(2, nc.gpsimd.tensor_tensor(r1, a1, minus_half[:], ALU.pow))
                step(3, nc.gpsimd.tensor_tensor(sq, r1, r1, ALU.mult))
                step(4, nc.gpsimd.tensor_tensor(v2, sq, var, ALU.mult))
                step(5, nc.gpsimd.tensor_scalar(a2, v2, BIT_EPS, None, ALU.add))
                step(6, nc.gpsimd.tensor_tensor(r2, a2, minus_half[:], ALU.pow))
                step(7, nc.gpsimd.tensor_tensor(rr, r1, r2, ALU.mult))
                step(8, nc.gpsimd.tensor_tensor(shift, mean, rr, ALU.mult))
                step(9, nc.gpsimd.tensor_tensor(norm_c[:], a2, r2, ALU.mult))
                nc.gpsimd.tensor_scalar(shift, shift, -1.0, None, ALU.mult).then_inc(ln_ready, 1)

            def norm_diagonals(b, first=False):
                pool.wait_ge(ln_ready, b + 1)
                alone(pool)
                for t in range(NT):
                    nc.gpsimd.tensor_scalar((first_c_diag if first else c_diag)[:, t, :], ident32[:], norm_c[:, t:t + 1], None,
                                            ALU.mult).then_inc(diag_ready, 1)

            def add_x(b):
                for t in range(NT):
                    pool.wait_ge(resid_dma[t % 2], b * 32 + 16 * (t // 2) + 16)
                    pool.wait_ge(scaled_ready, b * NT + t + 1)
                    nc.gpsimd.tensor_tensor(result[:, t, :], result[:, t, :], resid[:, t % 2, :], ALU.add).then_inc(result_ready, 1)

            def body(b, first=False, last=False):
                for pair in range(4):
                    for half in range(2):
                        pool.wait_ge(rot_hi_ready, b * 8 + 2 * pair + half + 1)
                        nc.gpsimd.tensor_tensor(split_buf[:, pair % 2, 2 + half, :], rope_sum[:, pair % 2, half, :],
                                                split_buf[:, pair % 2, half, :], ALU.subtract).then_inc(rot_lo_ready, 1)
                if not first:
                    add_x(b - 1)
                for f in range(1, FC):
                    pool.wait_ge(sq_ready, b * FC + f + 1)
                    if f >= 2:
                        pool.wait_ge(sq_added, b * (FC - 1) + f - 1)
                    nc.gpsimd.tensor_tensor(sq_sum[:], sq_sum[:], squares[:, f % 2, :], ALU.add).then_inc(sq_added, 1)
                pool.wait_ge(var_ready, b + 1)
                nc.gpsimd.tensor_tensor(ffn[:, 8, :], ffn[:, 5, :], minus_half[:], ALU.pow).then_inc(rstd_ready, 1)
                if not last:
                    normalise(b + 1)

                def mask(g):
                    for k in range(GH):
                        pool.wait_ge(probs_ready, b * H + GH * g + k + 1)
                        alone(pool)
                        head = probs[:, g % 2, k, :]
                        for blocks in (head[:, 0:1024].rearrange("p (j c) -> p j c", c=512)[:, :, 0:P],
                                       head[:, KEY_COLS[3]:KEY_COLS[3] + 2 * P].rearrange("p (j c) -> p j c", c=P)):
                            ins = nc.gpsimd.affine_select(blocks, blocks, [[0, 2], [1, P]], ALU.is_ge, 0.0, base=0, channel_multiplier=-1)
                        ins.then_inc(probs_masked, 1)

                def split_context(g):
                    pool.wait_ge(ctx_ready, b * NG + g + 1)
                    alone(pool)
                    nc.gpsimd.tensor_copy(ctxT[:, 0, g, :], ctx_f32[:, g % 2, :]).then_inc(ctx_hi, 1)
                    pool.wait_ge(ctx_hi, b * NG + g + 1)
                    nc.gpsimd.tensor_tensor(ctxT[:, 1, g, :], ctx_f32[:, g % 2, :], ctxT[:, 0, g, :], ALU.subtract).then_inc(ctx_lo, 1)

                mask(0)
                if not last:
                    norm_diagonals(b + 1)
                mask(1)
                mask(2)
                split_context(0)
                mask(3)
                for g in range(1, NG):
                    split_context(g)

            pool.wait_ge(w_max_ready, 3)
            nc.gpsimd.partition_all_reduce(scl[:, S_Q:S_Q + 3], w_all[:, 0:3], P, RMAX).then_inc(w_max_all, 1)
            normalise(0, first=True)
            norm_diagonals(0, first=True)
            for m in range(2):
                pool.wait_ge(w_abs_ready, m + 1)
                nc.gpsimd.partition_all_reduce(col(G_FC + m), w_all[:, 4 + m:5 + m], P, RADD).then_inc(w_abs_all, 1)
                pool.wait_ge(thresholds, m + 1)
                for k in range(m * n_tern // 2, (m + 1) * n_tern // 2):
                    if k >= 4:
                        pool.wait_ge(w_unit_ready, n_first + k - 3)
                    nc.gpsimd.tensor_scalar(below[:, (2 * k + 1) % 8, :], raw_parts(units[n_first + k])[1], col(MTHR + m), None,
                                            ALU.is_lt).then_inc(w_below_pool, 1)
            pool.wait_ge(w_max_ready, 4)
            nc.gpsimd.partition_all_reduce(col(S_O), w_all[:, 3:4], P, RMAX).then_inc(w_max_all, 1)
            body(0, first=True)
            with pool.Fori(1, NB - 1) as b:
                body(b)
            body(NB - 1, last=True)
            add_x(NB - 1)


_INS = ["L0_attn_x", "L0_attn_Wq", "L0_attn_Wk", "L0_attn_Wv", "L0_attn_Wo", "L0_ffn_w_fc", "L0_ffn_w_proj"]


def rope_tables():
    import numpy as np

    inv_freq = np.exp(np.float32(-np.log(10000.0)) * np.arange(0, DK, 2, dtype=np.float32) / np.float32(DK))
    angle = np.arange(S, dtype=np.float32)[None, :] * np.repeat(inv_freq.astype(np.float32), HS)[:, None]
    return [np.ascontiguousarray(f(angle).astype(np.float32) * np.float32(ROPE_SHRINK)) for f in (np.cos, np.sin)]


def kernel(**inputs):
    import numpy as _np
    import concourse.bacc as _bacc
    from concourse import mybir as _mybir
    from concourse.bass_utils import run_bass_kernel_spmd as _run

    nc = _bacc.Bacc("TRN2", target_bir_lowering=False, num_devices=1)
    arrays, args = {}, []
    named = [(name, _np.ascontiguousarray(inputs[name])) for name in _INS]
    named += list(zip(("rope_cos", "rope_sin"), rope_tables()))
    for name, a in named:
        arrays[f"in_{name}_dram"] = a
        args.append(nc.dram_tensor(f"in_{name}_dram", a.shape, _mybir.dt.from_np(a.dtype), kind="ExternalInput").ap())
    args.append(nc.dram_tensor("out_0_dram", (NB, S, D), F32, kind="ExternalOutput").ap())
    program(nc, *args)
    r = _run(nc, [arrays], core_ids=[0])
    return r.results[0]["out_0_dram"]
```

```python
from contextlib import ExitStack

import concourse.bass as bass
from concourse import mybir

F32 = mybir.dt.float32
F16 = mybir.dt.float16
BF16 = mybir.dt.bfloat16
ALU = mybir.AluOpType
ACT = mybir.ActivationFunctionType
AX_X = mybir.AxisListType.X
RMAX = bass.bass_isa.ReduceOp.max
RADD = bass.bass_isa.ReduceOp.add

P = 128
NB, S, D = 8, 512, 512
H, DK = 16, 32
NF = DK // 2
F = 4 * D
NT = S // P
ND = D // P
FC = F // P
HS = P // NF
GH = P // DK
NG = H // GH
KS = 3 * DK
KM = KS + 2
ROPE_SHRINK = 1.0 / 16
LN_EPS, BIT_EPS = 1e-5, 1e-6
MASKED = -1e30
KEY_COLS = [0, 512, 1024, 896]
PROBS = 1280
PER_ROUND = {3: 2, 2: 2, 1: 4, 0: 8}
ROUNDS = [(i, h, PER_ROUND[i]) for i in (3, 2, 1, 0) for h in range(0, H, PER_ROUND[i])]
NR = len(ROUNDS)
N_ABS = 8
ABS_ACT = 4
DOWN_MATMULS = 2 * FC
DOWN_BESIDE_SCORES = (NT - 1) * DOWN_MATMULS - 8
DOWN_BESIDE_EXP = 12
DOWN_BEFORE_MAXIMA = DOWN_BESIDE_SCORES + 10
X_BANKS = (3, 4, 5, 2)


def program(nc, x, w_q, w_k, w_v, w_o, w_fc, w_proj, rope_cos, rope_sin, out, norm_row):
    with ExitStack() as ctx:
        def sb(name, shape, dt):
            return ctx.enter_context(nc.sbuf_tensor(name, shape, dt))

        def sem(name):
            return ctx.enter_context(nc.semaphore(name))

        qkT = sb("qkT", [P, 2, 2, ND, 2, 2, P], F16)
        voT = sb("voT", [P, 2, 2, ND, D], F16)
        fcT = sb("fcT", [P, ND, F], F16)
        projT = sb("projT", [P, FC, D], F16)
        stacks = sb("stacks", [P, 2, H, S], F16)
        q_stack, k_stack = stacks[:, 0], stacks[:, 1]
        arena = sb("arena", [P, 2, GH, PROBS], F32)
        probs = arena[:]
        arena_f = arena[:].rearrange("p a b c -> p (a b c)")
        hid = arena_f[:, 0:8192].bitcast(F16).rearrange("p (s f t) -> p s f t", s=2, f=FC)
        rope_prods = arena_f[:, 8192:10240].rearrange("p (k t) -> p k t", k=4)
        result = rope_prods
        xr_buf = sb("xr_buf", [P, NT, D], F32)
        x_sb = xr_buf[:]
        rope_sum = xr_buf[:].rearrange("p (a b) t -> p a b t", a=2)
        xh_buf = sb("xh_buf", [P, NT, D], F32)
        xhat = xh_buf[:]
        gelu_out = xh_buf[:]
        xT = sb("xT", [P, 2, ND, S], F16)
        rope_tab = sb("rope_tab", [P, 2, S], F32)
        mix = sb("mix", [P, 2, S], F32)
        rope_row = mix[:]
        norm_rows = mix[:, 0, :]
        tanh_sb = xr_buf[:]
        row_max = mix[:, 0, 0:NT * H].rearrange("p (i h) -> p i h", i=NT)
        left_max = mix[:, 0, 256:256 + NT * H].rearrange("p (i h) -> p i h", i=NT)
        masked_scores = mix[:, 1, :].bitcast(BF16).rearrange("p (h k) -> p h k", h=8)
        max_parts = mix[:, 0, 64:128].bitcast(F16).rearrange("p (i s h) -> p i s h", i=NT, s=2)
        bn = mix[:, 0, 128:128 + 6 * NT].rearrange("p (t k) -> p t k", t=NT)
        maxT = mix[0:2 * H, 1, 0:S // 2].bitcast(F16)
        split_buf = sb("split_buf", [P, 2, 4, S], F16)
        split_f = split_buf[:].rearrange("p a b t -> p (a b t)").bitcast(F32)
        squares = split_f[:, 0:1024].rearrange("p (a t) -> p a t", a=2)
        ctx_f32 = split_f[:, 0:1024].rearrange("p (a t) -> p a t", a=2)
        inv_sums = split_f[:, 1024:1536]
        sq_sum = split_f[:, 1536:2048]
        v_sb = sb("v_sb", [P, NT, D], F32)
        ctxT = sb("ctxT", [P, 2, NG, S], F16)
        gate = sb("gate", [P, NT, D], F32)
        resid = sb("resid", [P, 2, D], F32)
        w_rowsum = sb("w_rowsum", [P, D], F16)
        ident16 = sb("ident16", [P, P], F16)
        ident32 = sb("ident32", [P, P], F32)
        mask_q = sb("mask_q", [P, P], BF16)
        ones32 = sb("ones32", [P, P], F32)
        ones16 = sb("ones16", [P, P], F16)
        mean_var = sb("mean_var", [P, NT, 2], F32)
        ln = sb("ln", [P, 8, NT], F32)
        norm_c = sb("norm_c", [P, NT], F32)
        minus_half = sb("minus_half", [P, NT], F32)
        ffn = sb("ffn", [P, 12, NT], F32)
        gate_scale = sb("gate_scale", [P, 2, NT], F32)
        w_part = ffn[:].rearrange("p k t -> p (k t)")[:, 0:2 * N_ABS]
        w_all = sb("w_all", [P, 6], F32)
        scl = sb("scl", [P, 20], F32)

        raw_attn = [gate[:], ctxT[:].rearrange("p a b t -> p (a b t)").bitcast(F32).rearrange("p (a t) -> p a t", a=ND),
                    v_sb[:], x_sb]
        raw_fc = stacks[:].rearrange("p a h t -> p (a h t)").bitcast(F32).rearrange("p (c d) -> p c d", c=FC)
        raw_proj = arena_f[:, 0:8192].rearrange("p (c d) -> p c d", c=ND)
        rings = [split_buf[:].rearrange("p a (b s) t -> p (a b) s t", s=2), ctxT[:].rearrange("p a (b s) t -> p (a b) s t", s=2)]
        below = gate[:].rearrange("p a t -> p (a t)").bitcast(F16).rearrange("p (a t) -> p a t", a=8)
        magnitudes = resid[:].rearrange("p a t -> p (a t)")

        banks = ctx.enter_context(nc.psum_tensor("banks", [P, 8, 512], F32))
        banks16 = banks[:].rearrange("p b c -> p (b c)").bitcast(F16).rearrange("p (b c) -> p b c", b=8)
        st_region = [banks[:, 0:3, :].rearrange("p b c -> p (b c)"), banks[:, 3:6, :].rearrange("p b c -> p (b c)")]

        w_dma = [sem(f"w_dma{i}") for i in range(6)]
        tab_dma, ones_dma = sem("tab_dma"), sem("ones_dma")
        stood_alone = sem("stood_alone")
        consts = sem("consts")
        w_max_ready, w_max_all = sem("w_max_ready"), sem("w_max_all")
        w_abs_part, w_abs_dve, w_abs_ready, w_abs_all = sem("w_abs_part"), sem("w_abs_dve"), sem("w_abs_ready"), sem("w_abs_all")
        attn_scl_step, ffn_scl_step = sem("attn_scl_step"), sem("ffn_scl_step")
        w_hi_ready, w_unit_ready = sem("w_hi_ready"), sem("w_unit_ready")
        w_below_pool, w_below_dve = sem("w_below_pool"), sem("w_below_dve")
        w_turned, w_kept = sem("w_turned"), sem("w_kept")
        thresholds = sem("thresholds")
        rowsum_ps, rowsum_kept = sem("rowsum_ps"), sem("rowsum_kept")
        x_dma, out_dma, max_dma = sem("x_dma"), sem("out_dma"), sem("max_dma")
        resid_dma = [sem("resid_dma0"), sem("resid_dma1")]
        stack_dma = [sem("stack_dma0"), sem("stack_dma1")]
        bn_ready, mv_ready, ln_step = sem("bn_ready"), sem("mv_ready"), sem("ln_step")
        xhat_ready, row_dma, rows_dma = sem("xhat_ready"), sem("row_dma"), sem("rows_dma")
        xT_ps, xhi_ready, xlo_ready = sem("xT_ps"), sem("xhi_ready"), sem("xlo_ready")
        rope_row_ready = sem("rope_row_ready")
        qk_ps, rope_prod_ready, rope_sum_ready = sem("qk_ps"), sem("rope_prod_ready"), sem("rope_sum_ready")
        rot_hi_ready, rot_lo_ready = sem("rot_hi_ready"), sem("rot_lo_ready")
        v_ps, v_ready = sem("v_ps"), sem("v_ready")
        wo_ps, scaled_ready, result_ready = sem("wo_ps"), sem("scaled_ready"), sem("result_ready")
        fc_ps, gelu_ready = sem("fc_ps"), sem("gelu_ready")
        hid_hi_ready, hid_lo_ready = sem("hid_hi_ready"), sem("hid_lo_ready")
        sq_ready, sq_added, sq_ps = sem("sq_ready"), sem("sq_added"), sem("sq_ps")
        down_ps, down_kept = sem("down_ps"), sem("down_kept")
        s_ps, max_ready, max_joined = sem("s_ps"), sem("max_ready"), sem("max_joined")
        max_hi, max_lo = sem("max_hi"), sem("max_lo")
        maxT_ps, maxT_ready = sem("maxT_ps"), sem("maxT_ready")
        sums_read, ffn_step, var_ready, rstd_ready = sem("sums_read"), sem("ffn_step"), sem("var_ready"), sem("rstd_ready")
        ln_ready = sem("ln_ready")
        centred, tanh_ready, gate_ready = sem("centred"), sem("tanh_ready"), sem("gate_ready")
        st_ps, probs_ready, probs_masked, pv_ps = sem("st_ps"), sem("probs_ready"), sem("probs_masked"), sem("pv_ps")
        pv_kept, inv_ready, ctx_ready = sem("pv_kept"), sem("inv_ready"), sem("ctx_ready")
        ctx_hi, ctx_lo = sem("ctx_hi"), sem("ctx_lo")

        S_Q, S_K, S_V, S_O, INV, EXP_SCALE, SVO = 0, 1, 2, 3, 4, 8, 9
        G_FC, G_PROJ, INV_G, THR, MTHR, BIT_EPS_G, HALF_GP = 10, 11, 12, 13, 15, 17, 18

        def col(c):
            return scl[:, c:c + 1]

        units = [("attn", m, o) for m in (2, 0, 1) for o in range(ND)]
        n_first = len(units)
        units += [("fc", o) for o in range(0, FC, 2)]
        units += [("proj", o, f) for o in range(ND) for f in range(0, 4, 2)]
        n_tern = len(units) - n_first
        units += [("attn", 3, o) for o in range(ND)]
        n_units = len(units)
        fu = [n_first + k for k in range(n_tern)]
        TURNS_AFTER_V = [[], [], [], fu[0:2]]
        TURNS_AFTER_QK = [fu[2:4], fu[4:5], fu[5:6], fu[6:8], [], fu[8:10], [], fu[10:12]]
        TURNS_IN_UP = fu[12:16]
        MADE_BEFORE_ROPE = fu[0:6]
        MADE_AFTER_ROPE = [fu[6:8], fu[8:10], fu[10:12], fu[12:16]]
        BELOW_BEFORE_ROPE = fu[0:8]
        BELOW_AFTER_ROPE = [fu[8:10], fu[10:12], fu[12:14], fu[14:16]]

        def turn_bank(u):
            if u < n_first:
                return (6, 7, 0, 1)[u % 4]
            return 6 + u % 2 if u < n_first + n_tern else 2 + u % 4

        def ring(u):
            return rings[u >= n_first][:, u % 4]

        def raw_parts(unit):
            if unit[0] == "fc":
                return [raw_fc[:, unit[1] + k, :] for k in range(2)]
            return [raw_proj[:, unit[1], (unit[2] + k) * 512:(unit[2] + k + 1) * 512] for k in range(2)]

        block = ctx.enter_context(nc.Block())

        def alone(eng):
            eng.sem_inc(stood_alone, 1)

        @block.sync
        def _(sp):
            def load_weight(raw, w, n):
                sp.dma_start(raw, w.rearrange("(c p) d -> p c d", p=P)).then_inc(w_dma[n], 16)

            load_weight(raw_attn[2], w_v, 2)
            sp.dma_start(x_sb, x[0].rearrange("(t p) d -> p t d", p=P)).then_inc(x_dma, 16)
            load_weight(raw_attn[0], w_q, 0)
            load_weight(raw_attn[1], w_k, 1)
            sp.dma_start(rope_tab[:, 0, :], rope_cos).then_inc(tab_dma, 16)
            sp.dma_start(rope_tab[:, 1, :], rope_sin).then_inc(tab_dma, 16)
            load_weight(raw_fc, w_fc, 4)
            load_weight(raw_proj, w_proj, 5)

            def load_resid(b, t):
                if t >= 2:
                    sp.wait_ge(result_ready, b * NT + t - 1)
                sp.dma_start(resid[:, t % 2, :], x[b].rearrange("(t p) d -> t p d", p=P)[t]).then_inc(resid_dma[t % 2], 16)

            def store_result(b):
                for t in range(NT):
                    sp.wait_ge(result_ready, b * NT + t + 1)
                    sp.dma_start(out[b].rearrange("(t p) d -> t p d", p=P)[t], result[:, t, :]).then_inc(out_dma, 16)
                    if t + 2 < NT:
                        load_resid(b, t + 2)

            def spread_norms(b):
                sp.wait_ge(ln_ready, b + 1)
                for t in range(NT):
                    sp.dma_start(norm_row[t * P:(t + 1) * P], norm_c[:, t:t + 1]).then_inc(row_dma, 16)
                sp.wait_ge(row_dma, b * NT * 16 + NT * 16)
                sp.dma_start(norm_rows, norm_row.partition_broadcast(P)).then_inc(rows_dma, 16)

            def body(b, first=False, last=False):
                if not first:
                    load_resid(b - 1, 0)
                    load_resid(b - 1, 1)
                else:
                    sp.wait_ge(w_kept, n_first + FC // 2)
                    sp.dma_start(k_stack[KS:KM, :, :], ones16[:]).then_inc(ones_dma, 16)
                for pair in range(4):
                    stack, heads = (q_stack, k_stack)[pair // 2], slice(HS * (pair % 2), HS * (pair % 2 + 1))
                    if pair == 0 and not first:
                        sp.wait_ge(st_ps, b * H)
                    sp.wait_ge(rot_lo_ready, b * 8 + 2 * pair + 2)
                    order = ((0, 0, 1), (0, 1, 0))[pair // 2]
                    for third, part in enumerate(order):
                        for half in range(2):
                            row = third * DK + half * NF
                            sp.dma_start(stack[row:row + NF, heads, :], split_buf[:, pair % 2, 2 * part + half, :]
                                         ).then_inc(stack_dma[pair % 2], 16)

                def load_next():
                    sp.dma_start(x_sb, x[b + 1].rearrange("(t p) d -> p t d", p=P)).then_inc(x_dma, 16)

                if first:
                    load_weight(raw_attn[3], w_o, 3)
                elif not last:
                    load_next()
                if not first:
                    store_result(b - 1)
                sp.wait_ge(maxT_ready, b + 1)
                sp.dma_start(q_stack[KS:KM, :, :], maxT[:, :]).then_inc(max_dma, 16)
                if first:
                    sp.wait_ge(w_unit_ready, n_units)
                    load_next()
                if not last:
                    spread_norms(b + 1)

            spread_norms(0)
            body(0, first=True)
            with sp.Fori(1, NB - 1) as b:
                body(b)
            body(NB - 1, last=True)
            load_resid(NB - 1, 0)
            load_resid(NB - 1, 1)
            store_result(NB - 1)
            sp.wait_ge(out_dma, NB * NT * 16)

        @block.tensor
        def _(pe):
            pe.wait_ge(consts, 1)

            def turn_weights(first, end):
                for u in range(first, end):
                    pe.wait_ge(w_unit_ready, u + 1)
                    if u < n_first and u >= 4:
                        pe.wait_ge(w_kept, u - 3)
                    if n_first + 2 <= u < n_first + n_tern:
                        pe.wait_ge(w_kept, u - 1)
                    for k in range(8):
                        mm = pe.transpose(banks16[:, turn_bank(u), k * P:(k + 1) * P],
                                          ring(u)[:, k // 4, (k % 4) * P:(k % 4 + 1) * P], ident16[:])
                    mm.then_inc(w_turned, 1)

            def ternary_row_sums():
                pe.wait_ge(w_kept, n_first + n_tern)
                for f in range(FC):
                    mm = pe.matmul(banks[:, 7, :], ones16[:], projT[:, f, :], start=(f == 0), stop=(f == FC - 1))
                mm.then_inc(rowsum_ps, 1)

            def three_products(out_ap, hi_lo, n, key):
                for c in range(n):
                    for k, (a, r) in enumerate(((0, 0), (0, 1), (1, 0))):
                        lhs, rhs = hi_lo(a, r, c)
                        mm = pe.matmul(out_ap, lhs, rhs, start=(c == 0 and k == 0), stop=(c == n - 1 and k == 2))
                return mm

            def out_projection(b):
                for t in range(NT):
                    if t == 0:
                        pe.wait_ge(ctx_lo, b * NG + NG)
                    if t >= 2:
                        pe.wait_ge(scaled_ready, b * NT + t - 1)
                    three_products(banks[:, 6 + t % 2, :],
                                   lambda a, r, c: (ctxT[:, a, c, t * P:(t + 1) * P], voT[:, 1, r, c, :]),
                                   NG, "o").then_inc(wo_ps, 1)

            def turn_tokens(b, t, first=False):
                if t == 0 and not first:
                    pe.wait_ge(probs_ready, b * H - 1)
                if t == 3 and not first:
                    pe.wait_ge(probs_ready, b * H)
                pe.wait_ge(xhat_ready, b * NT + t + 1)
                for c in range(ND):
                    mm = pe.transpose(banks[:, X_BANKS[t], c * P:(c + 1) * P], xhat[:, t, c * P:(c + 1) * P], ident32[:])
                mm.then_inc(xT_ps, 1)

            def last_out_projection(b):
                for last in (0, 1):
                    pe.wait_ge(ctx_lo, b * NG + NG - 1 + last)
                    for t in range(NT):
                        for c in (range(NG - 1), range(NG - 1, NG))[last]:
                            for k, (a, r) in enumerate(((0, 0), (0, 1), (1, 0))):
                                mm = pe.matmul(banks[:, t, :], ctxT[:, a, c, t * P:(t + 1) * P], voT[:, 1, r, c, :],
                                               start=(c == 0 and k == 0), stop=(c == NG - 1 and k == 2))
                        if last:
                            mm.then_inc(wo_ps, 1)

            def body(b, first=False, last=False):
                for t in range(NT):
                    pe.wait_ge(xlo_ready, b * NT + t + 1)
                    if t == 0 and first:
                        pe.wait_ge(w_kept, n_first)
                    if t >= 2:
                        pe.wait_ge(v_ready, b * NT + t - 1)
                    three_products(banks[:, t % 2, :],
                                   lambda a, r, c: (xT[:, a, c, t * P:(t + 1) * P], voT[:, 0, r, c, :]),
                                   ND, "v").then_inc(v_ps, 1)
                    for u in TURNS_AFTER_V[t] if first else []:
                        turn_weights(u, u + 1)
                for pair in range(4):
                    if pair >= 2:
                        pe.wait_ge(rope_prod_ready, b * 16 + 4 * (pair - 2) + 4)
                    for half in range(2):
                        three_products(banks[:, 2 + 2 * (pair % 2) + half, :],
                                       lambda a, r, c: (qkT[:, pair // 2, r, c, pair % 2, half, :], xT[:, a, c, :]),
                                       ND, "qk").then_inc(qk_ps, 1)
                        for u in TURNS_AFTER_QK[2 * pair + half] if first else []:
                            turn_weights(u, u + 1)
                if not first:
                    out_projection(b - 1)
                for f in range(FC):
                    if f < 2:
                        pe.wait_ge(v_ready, b * NT + 3 + f)
                    else:
                        pe.wait_ge(gelu_ready, b * FC + f - 1)
                    for c in range(ND):
                        for part in range(2):
                            mm = pe.matmul(banks[:, f % 2, :], fcT[:, c, f * P:(f + 1) * P], xT[:, part, c, :],
                                           start=(c == 0 and part == 0), stop=(c == ND - 1 and part == 1))
                    mm.then_inc(fc_ps, 1)
                    for u in TURNS_IN_UP if first and f == 1 else []:
                        turn_weights(u, u + 1)

                def down():
                    for t in range(NT):
                        if t == 0:
                            if not first:
                                pe.wait_ge(scaled_ready, b * NT)
                            pe.wait_ge(gelu_ready, b * FC + FC)
                        if t == 1 and first:
                            pe.wait_ge(rowsum_kept, 1)
                        if t >= 2:
                            pe.wait_ge(down_kept, b * 2 + t - 1)
                        order = [(f, part) for f in range(FC) for part in range(2)]
                        if t == NT - 1:
                            order = [(f, part) for part in range(2) for f in range(FC)]
                        for f, part in order:
                            if t == 0 and part == 0:
                                pe.wait_ge(hid_lo_ready, b * FC + f + 1)
                            lhs = hid[:, part, f, t * P:(t + 1) * P]
                            ends = dict(start=(f == 0 and part == 0), stop=(f == FC - 1 and part == 1))
                            if t < NT - 1:
                                pe.matmul(banks[:, 0, t:t + 1], lhs, ones16[:, 0:1], **ends)
                            mm = pe.matmul(banks[:, 6 + t % 2, :], lhs, projT[:, f, :], **ends)
                            if ends["stop"]:
                                mm.then_inc(down_ps, 1)
                            yield

                if first:
                    ternary_row_sums()
                downs = down()
                given = 0
                for r, (i, h0, n) in enumerate(ROUNDS):
                    if r == 0:
                        for s in stack_dma:
                            pe.wait_ge(s, (b + 1) * 192)
                        pe.wait_ge(rope_prod_ready, b * 16 + 16)
                    if r >= 2:
                        pe.wait_ge(max_ready, b * NR + r - 1)
                    keys = (i + 1) * P
                    per_bank = 512 // keys
                    for k in range(n):
                        bank, at = 2 + 2 * (r % 2) + k // per_bank, (k % per_bank) * keys
                        mm = pe.matmul(banks[:, bank, at:at + keys], q_stack[0:KS, h0 + k, i * P:(i + 1) * P],
                                       k_stack[0:KS, h0 + k, 0:keys], start=True, stop=True)
                    mm.then_inc(s_ps, 1)
                    while given < DOWN_BESIDE_SCORES * (r + 1) // NR:
                        next(downs)
                        given += 1
                while given < DOWN_BEFORE_MAXIMA:
                    next(downs)
                    given += 1
                pe.wait_ge(max_lo, b + 1)
                for i in range(NT):
                    mm = pe.transpose(banks16[0:2 * H, 1, i * P:(i + 1) * P],
                                      max_parts[:, i].rearrange("p s h -> p (s h)"), ident16[:])
                mm.then_inc(maxT_ps, 1)
                for f in range(FC):
                    for part in range(2):
                        pe.matmul(banks[:, 0, NT - 1:NT], hid[:, part, f, S - P:S], ones16[:, 0:1],
                                  start=(f == 0 and part == 0), stop=(f == FC - 1 and part == 1))
                pe.wait_ge(sq_added, b * (FC - 1) + FC - 1)
                for t in range(NT):
                    mm = pe.matmul(banks[:, 0, NT + t:NT + t + 1], sq_sum[:, t * P:(t + 1) * P], ones32[:, 0:1], start=True, stop=True)
                mm.then_inc(sq_ps, 1)
                while given < NT * DOWN_MATMULS - DOWN_BESIDE_EXP:
                    next(downs)
                    given += 1

                if first:
                    turn_weights(n_first + n_tern, n_units)
                def scores(h):
                    if h == 0 and first:
                        pe.wait_ge(w_kept, n_units)
                        pe.wait_ge(ones_dma, 16)
                    if h == 0:
                        pe.wait_ge(max_dma, (b + 1) * 16)
                    if h == 1:
                        pe.wait_ge(sums_read, b + 1)
                    if h >= 2:
                        pe.wait_ge(probs_ready, b * H + h - 1)
                    ps = st_region[(h + 1) % 2]
                    for j in (0, 1, 3, 2):
                        at, n = KEY_COLS[j], S - j * P
                        mm = pe.matmul(ps[:, at:at + n], k_stack[0:KM, h, j * P:(j + 1) * P], q_stack[0:KM, h, j * P:S],
                                       start=True, stop=True)
                    mm.then_inc(st_ps, 1)

                def weigh(g, j):
                    if j == 0:
                        pe.wait_ge(probs_masked, 2 * (b * H + GH * (g + 1)) - 1)
                    if j == 2:
                        pe.wait_ge(probs_masked, 2 * (b * H + GH * (g + 1)))
                    if j == 0:
                        if g == 0:
                            pe.wait_ge(centred, b * NT + NT)
                        else:
                            pe.wait_ge(pv_kept, (b * NG + g) * 2 - 1)
                    at, n = KEY_COLS[j], S - j * P
                    for bank in (6, 7):
                        if j == 0 and g > 0 and bank == 7:
                            pe.wait_ge(pv_kept, (b * NG + g) * 2)
                        for k in range(GH):
                            head = GH * g + k
                            lhs = v_sb[:, j, head * DK:(head + 1) * DK] if bank == 6 else ones32[:, 0:DK]
                            mm = pe.matmul(banks[k * DK:(k + 1) * DK, bank, j * P:S], lhs, probs[:, g % 2, k, at:at + n],
                                           start=(j == 0), stop=(j == NT - 1), tile_position=(0, k * DK))
                    if j == NT - 1:
                        mm.then_inc(pv_ps, 1)

                for g in range(NG + 1):
                    for k in range(GH):
                        if g < NG:
                            scores(GH * g + k)
                        for _ in range(4):
                            if g == 0:
                                next(downs, None)
                        if g > 0 and k > 0:
                            weigh(g - 1, k - 1)
                        if g == NG and not last:
                            if k == 0:
                                for t in range(3):
                                    turn_tokens(b + 1, t)
                            if k == 1:
                                turn_tokens(b + 1, 3)
                    if g > 0:
                        weigh(g - 1, NT - 1)

            turn_weights(0, ND)
            for t in range(NT):
                turn_tokens(0, t, first=True)
            turn_weights(ND, n_first)
            body(0, first=True)
            with pe.Fori(1, NB - 1) as b:
                body(b)
            body(NB - 1, last=True)
            last_out_projection(NB - 1)

        @block.scalar
        def _(act):
            def keep_weights(u):
                unit = units[u]
                act.wait_ge(w_turned, u + 1)
                src = banks16[:, turn_bank(u), :]
                if unit[0] == "fc":
                    dst = fcT[:, :, unit[1] * P:(unit[1] + 2) * P].rearrange("p c (o n) -> p o c n", o=2)
                    mm = nc.scalar.copy(dst, src.rearrange("p (o c n) -> p o c n", o=2, c=ND))
                elif unit[0] == "proj":
                    _, o, f = unit
                    mm = nc.scalar.copy(projT[:, 4 * f:4 * f + 8, o * P:(o + 1) * P], src.rearrange("p (f n) -> p f n", f=8))
                else:
                    _, m, o = unit
                    src = src.rearrange("p (s c n) -> p s c n", s=2, c=ND)
                    if m >= 2:
                        mm = nc.scalar.copy(voT[:, m - 2, :, :, o * P:(o + 1) * P], src)
                    for part, half in [(p, h) for p in range(2) for h in range(2)] if m < 2 else []:
                        part_src = src[:, part].rearrange("p c (h f two) -> p c f h two", h=GH, two=2)[:, :, :, :, half]
                        dst = qkT[:, m, part, :, o // 2, half, :].rearrange("p c (f h) -> p c f h", h=HS)
                        mm = nc.scalar.copy(dst[:, :, :, GH * (o % 2):GH * (o % 2) + GH], part_src)
                mm.then_inc(w_kept, 1)

            def sum_magnitudes(m, k):
                raw = (raw_fc, raw_proj)[m].rearrange("p c d -> p (c d)")
                width = F * D // P // N_ABS
                act.wait_ge(w_dma[4 + m], 16)
                if m or k:
                    act.wait_ge(w_abs_part, ABS_ACT * m + k)
                nc.scalar.activation(magnitudes, raw[:, k * width:(k + 1) * width], ACT.Abs,
                                     accum_out=w_part[:, N_ABS * m + k:N_ABS * m + k + 1]).then_inc(w_abs_part, 1)

            def normalise(b, t):
                act.wait_ge(ln_ready, b + 1)
                nc.scalar.activation(xhat[:, t, :], x_sb[:, t, :], ACT.Identity, scale=ln[:, 6, t:t + 1],
                                     bias=ln[:, 7, t:t + 1]).then_inc(xhat_ready, 1)

            def split_tokens(b):
                for t in range(NT):
                    act.wait_ge(xT_ps, b * NT + t + 1)
                    nc.scalar.copy(xT[:, 0, :, t * P:(t + 1) * P],
                                   banks[:, X_BANKS[t], :].rearrange("p (c n) -> p c n", c=ND)).then_inc(xhi_ready, 1)

            for u in range(n_first):
                keep_weights(u)
                if u == ND - 1:
                    for t in range(NT):
                        normalise(0, t)
            split_tokens(0)
            for k in range(ABS_ACT):
                sum_magnitudes(0, k)

            def body(b, first=False, last=False):
                for t in range(NT):
                    act.wait_ge(v_ps, b * NT + t + 1)
                    nc.scalar.activation(v_sb[:, t, :], banks[:, t % 2, :], ACT.Copy, scale=norm_c[:, t:t + 1]).then_inc(v_ready, 1)
                    if first:
                        sum_magnitudes(1, t)
                for k, u in enumerate(MADE_BEFORE_ROPE if first else []):
                    keep_weights(u)
                    if NT + k < N_ABS:
                        sum_magnitudes(1, NT + k)

                for pair in range(4):
                    for half in range(2):
                        act.wait_ge(rope_sum_ready, b * 8 + 2 * pair + half + 1)
                        if half == 0 and pair >= 2:
                            act.wait_ge(stack_dma[pair % 2], b * 192 + 96)
                        if half == 0 and pair == 0 and not first:
                            act.wait_ge(ctx_lo, b * NG)
                        nc.scalar.copy(split_buf[:, pair % 2, half, :], rope_sum[:, pair % 2, half, :]).then_inc(rot_hi_ready, 1)
                    for u in MADE_AFTER_ROPE[pair] if first and pair < 3 else []:
                        keep_weights(u)

                nc.scalar.preload_act_table(ACT.Gelu)

                def square(f):
                    act.wait_ge(gelu_ready, b * FC + f + 1)
                    if f == 0:
                        for s in stack_dma:
                            act.wait_ge(s, (b + 1) * 192)
                    if f >= 3:
                        act.wait_ge(sq_added, b * (FC - 1) + f - 2)
                    dst = sq_sum[:] if f == 0 else squares[:, f % 2, :]
                    nc.scalar.activation(dst, gelu_out[:, f % 4, :], ACT.Square, scale=col(INV_G)).then_inc(sq_ready, 1)

                for f in range(FC):
                    act.wait_ge(fc_ps, b * FC + f + 1)
                    if f >= 4:
                        act.wait_ge(hid_lo_ready, b * FC + f - 3)
                        act.wait_ge(sq_ready, b * FC + f - 3)
                    nc.scalar.activation(gelu_out[:, f % 4, :], banks[:, f % 2, :], ACT.Gelu, scale=col(G_FC)).then_inc(gelu_ready, 1)
                    for u in TURNS_IN_UP if first and f == 0 else []:
                        keep_weights(u)
                    if f >= 1:
                        square(f - 1)
                square(FC - 1)
                if first:
                    act.wait_ge(rowsum_ps, 1)
                    nc.scalar.copy(w_rowsum[:], banks[:, 7, :]).then_inc(rowsum_kept, 1)
                for t in range(2):
                    act.wait_ge(down_ps, b * NT + t + 1)
                    nc.scalar.copy(gate[:, t, :], banks[:, 6 + t % 2, :]).then_inc(down_kept, 1)

                for u in range(n_first + n_tern, n_units) if first else []:
                    keep_weights(u)
                nc.scalar.preload_act_table(ACT.Exp)
                for h in range(H):
                    g = h // GH
                    act.wait_ge(st_ps, b * H + h + 1)
                    if h % GH == 0 and g == 1 and not first:
                        act.wait_ge(out_dma, b * NT * 16)
                    if h % GH == 0 and g >= 2:
                        act.wait_ge(pv_ps, b * NG + g - 1)
                    nc.scalar.activation(probs[:, g % 2, h % GH, :], st_region[(h + 1) % 2][:, 0:PROBS], ACT.Exp,
                                         scale=col(EXP_SCALE)).then_inc(probs_ready, 1)
                    at = h - (8 if first else 4)
                    if not last and at % 2 == 1 and 0 < at < 2 * NT:
                        normalise(b + 1, at // 2)
                if not last:
                    split_tokens(b + 1)
                for t in range(NT):
                    act.wait_ge(centred, b * NT + NT)
                    nc.scalar.activation(tanh_sb[:, t, :], gate[:, t, :], ACT.Tanh,
                                         scale=gate_scale[:, 0, t:t + 1]).then_inc(tanh_ready, 1)

            body(0, first=True)
            with act.Fori(1, NB - 1) as b:
                body(b)
            body(NB - 1, last=True)

        @block.vector
        def _(dve):
            def largest(m):
                dve.wait_ge(w_dma[m], 16)
                nc.vector.tensor_reduce(w_all[:, m:m + 1], raw_attn[m].rearrange("p c d -> p (c d)"), AX_X, ALU.max,
                                        apply_absolute_value=True).then_inc(w_max_ready, 1)

            def attn_step(k, ins):
                ins.then_inc(attn_scl_step, 1)
                dve.wait_ge(attn_scl_step, k)

            def split_weights(u):
                _, m, o = units[u]
                if 4 <= u:
                    dve.wait_ge(w_turned, u - 3)
                nc.vector.tensor_scalar(ring(u)[:, 0, :], raw_attn[m][:, o, :], col(INV + m), None, ALU.mult).then_inc(w_hi_ready, 1)
                dve.wait_ge(w_hi_ready, u + 1 if u < n_first else u + 1 - n_tern)
                nc.vector.scalar_tensor_tensor(ring(u)[:, 1, :], raw_attn[m][:, o, :], col(INV + m), ring(u)[:, 0, :],
                                               ALU.mult, ALU.subtract).then_inc(w_unit_ready, 1)

            def ffn_scales(m):
                def step(k, ins):
                    ins.then_inc(ffn_scl_step, 1)
                    dve.wait_ge(ffn_scl_step, 4 * m + k)

                dve.wait_ge(w_abs_part, N_ABS * m + ABS_ACT)
                if m == 0:
                    dve.wait_ge(w_abs_dve, N_ABS - ABS_ACT)
                nc.vector.tensor_reduce(w_all[:, 4 + m:5 + m], w_part[:, N_ABS * m:N_ABS * (m + 1)], AX_X, ALU.add).then_inc(w_abs_ready, 1)
                dve.wait_ge(w_abs_all, m + 1)
                gamma = col(G_FC + m)
                step(1, nc.vector.tensor_scalar(gamma, gamma, 1.0 / (F * D), None, ALU.mult))
                step(2, nc.vector.tensor_scalar(col(THR + m), gamma, BIT_EPS, 0.5, ALU.add, ALU.mult))
                if m == 0:
                    step(3, nc.vector.reciprocal(col(INV_G), gamma))
                    step(4, nc.vector.scalar_tensor_tensor(col(BIT_EPS_G), col(INV_G), BIT_EPS, col(INV_G), ALU.mult, ALU.mult))
                else:
                    step(3, nc.vector.tensor_scalar(col(HALF_GP), gamma, 0.5, None, ALU.mult))
                nc.vector.tensor_scalar(col(MTHR + m), col(THR + m), -1.0, None, ALU.mult).then_inc(thresholds, 1)
                dve.wait_ge(thresholds, m + 1)

            def ternary(u):
                k, m, parts = u - n_first, int(units[u][0] == "proj"), raw_parts(units[u])
                nc.vector.tensor_scalar(below[:, 2 * k % 8, :], parts[0], col(MTHR + m), None, ALU.is_lt).then_inc(w_below_dve, 1)
                dve.wait_ge(w_turned, u - 3 if k >= 4 else n_first)
                dve.wait_ge(w_below_pool, k + 1)
                nc.vector.scalar_tensor_tensor(ring(u)[:, 1, :], parts[1], col(THR + m), below[:, (2 * k + 1) % 8, :],
                                               ALU.is_gt, ALU.subtract)
                dve.wait_ge(w_below_dve, k + 1)
                nc.vector.scalar_tensor_tensor(ring(u)[:, 0, :], parts[0], col(THR + m), below[:, 2 * k % 8, :],
                                               ALU.is_gt, ALU.subtract).then_inc(w_unit_ready, 1)

            def out_weights():
                largest(3)
                dve.wait_ge(w_max_all, 4)
                attn_step(8, nc.vector.tensor_scalar(col(S_O), col(S_O), 1e-30, None, ALU.max))
                attn_step(9, nc.vector.tensor_tensor(col(SVO), col(S_V), col(S_O), ALU.mult))
                attn_step(10, nc.vector.reciprocal(col(INV + 3), col(S_O)))
                for u in range(n_first + n_tern, n_units):
                    split_weights(u)

            def first_weights():
                largest(2)
                statistics(0)
                for k, m in enumerate((2, 0, 1)):
                    if k == 1:
                        largest(0)
                        largest(1)
                    dve.wait_ge(w_max_all, k + 1)
                    attn_step(2 * k + 1, nc.vector.tensor_scalar(col(m), col(m), 1e-30, None, ALU.max))
                    attn_step(2 * k + 2, nc.vector.reciprocal(col(INV + m), col(m)))
                    for u in range(k * ND, (k + 1) * ND):
                        split_weights(u)
                attn_step(7, nc.vector.scalar_tensor_tensor(col(EXP_SCALE), col(S_Q), DK ** -0.5 / ROPE_SHRINK ** 2, col(S_K),
                                                            ALU.mult, ALU.mult))
                width = F * D // P // N_ABS
                dve.wait_ge(w_dma[4], 16)
                for k in range(ABS_ACT, N_ABS):
                    nc.vector.tensor_reduce(w_part[:, k:k + 1], raw_fc.rearrange("p c d -> p (c d)")[:, k * width:(k + 1) * width],
                                            AX_X, ALU.add, apply_absolute_value=True).then_inc(w_abs_dve, 1)

            def statistics(b):
                dve.wait_ge(x_dma, b * 16 + 16)
                for t in range(NT):
                    nc.vector.bn_stats(bn[:, t, :], x_sb[:, t, :]).then_inc(bn_ready, 1)
                dve.wait_ge(bn_ready, b * NT + NT)
                alone(dve)
                for t in range(NT):
                    nc.vector.bn_aggr(mean_var[:, t, :], bn[:, t, :]).then_inc(mv_ready, 1)

            def finish_context(b, g, count):
                dve.wait_ge(pv_kept, count * 2)
                nc.vector.reciprocal(inv_sums, inv_sums).then_inc(inv_ready, 1)
                dve.wait_ge(inv_ready, count)
                nc.vector.tensor_tensor(ctx_f32[:, g % 2, :], ctx_f32[:, g % 2, :], inv_sums, ALU.mult).then_inc(ctx_ready, 1)

            def scale_by_gate(b, sums, final=False):
                dve.wait_ge(rope_sum_ready, sums)
                if final:
                    dve.wait_ge(gate_ready, b * NT + NT)
                for t in range(NT):
                    dve.wait_ge(wo_ps, b * NT + t + 1)
                    nc.vector.scalar_tensor_tensor(result[:, t, :], banks[:, t if final else 6 + t % 2, :], gate_scale[:, 1, t:t + 1],
                                                   gate[:, t, :], ALU.mult, ALU.mult).then_inc(scaled_ready, 1)

            def split_tokens(b, first=False):
                for t in range(NT):
                    dve.wait_ge(xhi_ready, b * NT + t + 1)
                    tile = xT[:, :, :, t * P:(t + 1) * P]
                    nc.vector.tensor_tensor(tile[:, 1], banks[:, X_BANKS[t], :].rearrange("p (c n) -> p c n", c=ND), tile[:, 0],
                                            ALU.subtract).then_inc(xlo_ready, 1)
                if first:
                    dve.wait_ge(tab_dma, 32)
                dve.wait_ge(rows_dma, b * 16 + 16)
                for k in (1, 0):
                    nc.vector.tensor_tensor(rope_row[:, k, :], norm_rows, rope_tab[:, k, :], ALU.mult).then_inc(rope_row_ready, 1)

            def body(b, first=False, last=False):
                if first:
                    ffn_scales(0)
                    for u in MADE_BEFORE_ROPE:
                        ternary(u)
                dve.wait_ge(rope_row_ready, b * 2 + 2)
                for pair in range(4):
                    if pair == 0 and not first:
                        dve.wait_ge(gate_ready, b * NT)
                    if pair >= 1:
                        dve.wait_ge(rope_sum_ready, b * 8 + 2 * pair)
                    dve.wait_ge(qk_ps, b * 8 + 2 * pair + 2)
                    for k, (half, table) in enumerate(((0, 0), (1, 1), (0, 1), (1, 0))):
                        nc.vector.tensor_tensor(rope_prods[:, k, :], banks[:, 2 + 2 * (pair % 2) + half, :], rope_row[:, table, :],
                                                ALU.mult).then_inc(rope_prod_ready, 1)
                    if pair >= 2:
                        dve.wait_ge(rot_lo_ready, b * 8 + 2 * (pair - 2) + 2)
                    dve.wait_ge(rope_prod_ready, b * 16 + 4 * pair + 4)
                    for half, op in enumerate((ALU.subtract, ALU.add)):
                        nc.vector.tensor_tensor(rope_sum[:, pair % 2, half, :], rope_prods[:, 2 * half, :], rope_prods[:, 2 * half + 1, :],
                                                op).then_inc(rope_sum_ready, 1)
                    for u in MADE_AFTER_ROPE[pair] if first else []:
                        ternary(u)
                    if pair == 0 and first:
                        ffn_scales(1)
                if not first:
                    scale_by_gate(b - 1, b * 8 + 8)
                if first:
                    dve.wait_ge(w_unit_ready, n_first + n_tern)
                for f in range(FC):
                    dve.wait_ge(gelu_ready, b * FC + f + 1)
                    nc.vector.tensor_scalar(hid[:, 0, f, :], gelu_out[:, f % 4, :], col(INV_G), None, ALU.mult).then_inc(hid_hi_ready, 1)
                    dve.wait_ge(hid_hi_ready, b * FC + f + 1)
                    nc.vector.scalar_tensor_tensor(hid[:, 1, f, :], gelu_out[:, f % 4, :], col(INV_G), hid[:, 0, f, :],
                                                   ALU.mult, ALU.subtract).then_inc(hid_lo_ready, 1)
                for r, (i, h0, n) in enumerate(ROUNDS):
                    if r == 0:
                        dve.wait_ge(hid_lo_ready, b * FC + FC)
                    dve.wait_ge(s_ps, b * NR + r + 1)
                    keys = (i + 1) * P
                    src = banks[:, 2 + 2 * (r % 2):4 + 2 * (r % 2), 0:512 // keys * keys].rearrange("p b (h k) -> p b h k", k=keys)
                    if i > 0:
                        out = left_max[:, i, h0:h0 + n].rearrange("p (b h) -> p b h", b=2)
                        nc.vector.tensor_reduce(out, src[:, :, :, 0:i * P], AX_X, ALU.max)
                    used = [q for q in range(r) if any(h % 8 in range(h0 % 8, h0 % 8 + n) for h in range(ROUNDS[q][1], ROUNDS[q][1] + ROUNDS[q][2]))]
                    if used:
                        dve.wait_ge(max_ready, b * NR + used[-1] + 1)
                    alone(dve)
                    for k in range(n):
                        block = src[:, k // (n // 2), k % (n // 2), i * P:keys]
                        ins = nc.vector.tensor_tensor_reduce(masked_scores[:, (h0 + k) % 8, :], block, mask_q[:], 1.0, MASKED,
                                                             ALU.add, ALU.max, row_max[:, i, h0 + k:h0 + k + 1])
                    ins.then_inc(max_ready, 1)
                dve.wait_ge(max_ready, b * NR + NR)
                nc.vector.tensor_tensor(row_max[:, 1:NT, :], row_max[:, 1:NT, :], left_max[:, 1:NT, :], ALU.max).then_inc(max_joined, 1)
                dve.wait_ge(max_joined, b + 1)
                nc.vector.tensor_scalar(max_parts[:, :, 0, :], row_max[:], -1.0, None, ALU.mult).then_inc(max_hi, 1)
                dve.wait_ge(max_hi, b + 1)
                nc.vector.scalar_tensor_tensor(max_parts[:, :, 1, :], row_max[:], -1.0, max_parts[:, :, 0, :],
                                               ALU.mult, ALU.subtract).then_inc(max_lo, 1)
                if not first:
                    dve.wait_ge(max_dma, b * 16)
                dve.wait_ge(maxT_ps, b + 1)
                nc.vector.tensor_copy(maxT[:, :], banks16[0:2 * H, 1, 0:S]).then_inc(maxT_ready, 1)
                if first:
                    out_weights()
                elif not last:
                    statistics(b + 1)
                mean, ex2 = ffn[:, 0, :], ffn[:, 1, :]
                neg_mean, msq, var, var_eps = (ffn[:, k, :] for k in range(2, 6))
                var_inv, nan_if_0, rstd, half_scale = (ffn[:, k, :] for k in range(6, 10))
                dve.wait_ge(sq_ps, b + 1)
                nc.vector.tensor_scalar(ffn[:, 0:2, :].rearrange("p k t -> p (k t)"), banks[:, 0, 0:2 * NT], 1.0 / F, None,
                                        ALU.mult).then_inc(sums_read, 1)
                dve.wait_ge(sums_read, b + 1)
                n_step = 7

                def step(k, ins):
                    ins.then_inc(ffn_step, 1)
                    dve.wait_ge(ffn_step, b * n_step + k)

                step(1, nc.vector.tensor_tensor(msq, mean, mean, ALU.mult))
                step(2, nc.vector.tensor_tensor(var, ex2, msq, ALU.subtract))
                nc.vector.tensor_scalar(var_eps, var, col(BIT_EPS_G), None, ALU.add).then_inc(var_ready, 1)
                step(3, nc.vector.tensor_scalar(neg_mean, mean, -1.0, None, ALU.mult))
                step(4, nc.vector.reciprocal(var_inv, var))
                step(5, nc.vector.tensor_tensor(nan_if_0, var, var_inv, ALU.mult))
                dve.wait_ge(rstd_ready, b + 1)
                step(6, nc.vector.scalar_tensor_tensor(gate_scale[:, 0, :], rstd, col(HALF_GP), nan_if_0, ALU.mult, ALU.mult))
                step(7, nc.vector.tensor_scalar(gate_scale[:, 1, :], gate_scale[:, 0, :], col(SVO), None, ALU.mult))
                for t in range(NT):
                    if t < 2:
                        dve.wait_ge(down_kept, b * 2 + t + 1)
                    else:
                        dve.wait_ge(down_ps, b * NT + t + 1)
                    nc.vector.scalar_tensor_tensor(gate[:, t, :], w_rowsum[:], neg_mean[:, t:t + 1],
                                                   gate[:, t, :] if t < 2 else banks[:, 6 + t % 2, :],
                                                   ALU.mult, ALU.add).then_inc(centred, 1)
                if first:
                    statistics(1)

                def keep_context(g):
                    if g >= 1:
                        dve.wait_ge(ctx_ready, b * NG + g)
                    if g >= 2:
                        dve.wait_ge(ctx_lo, b * NG + g - 1)
                    dve.wait_ge(pv_ps, b * NG + g + 1)
                    nc.vector.tensor_copy(ctx_f32[:, g % 2, :], banks[:, 6, :]).then_inc(pv_kept, 1)
                    nc.vector.tensor_copy(inv_sums, banks[:, 7, :]).then_inc(pv_kept, 1)

                def finish_gate(t):
                    dve.wait_ge(tanh_ready, b * NT + t + 1)
                    nc.vector.scalar_tensor_tensor(gate[:, t, :], tanh_sb[:, t, :], 1.0, gate[:, t, :],
                                                   ALU.add, ALU.mult).then_inc(gate_ready, 1)

                for g in range(NG):
                    keep_context(g)
                    if g == 2 and not last:
                        split_tokens(b + 1)
                    finish_context(b, g, b * NG + g + 1)
                for t in range(NT):
                    finish_gate(t)

            first_weights()
            split_tokens(0, first=True)
            body(0, first=True)
            with dve.Fori(1, NB - 1) as b:
                body(b)
            body(NB - 1, last=True)
            scale_by_gate(NB - 1, NB * 8, final=True)

        @block.gpsimd
        def _(pool):
            nc.gpsimd.memset(ones32[:], 1.0)
            nc.gpsimd.memset(ones16[:], 1.0)
            nc.gpsimd.memset(ident16[:], 0.0)
            nc.gpsimd.memset(ident32[:], 0.0)
            nc.gpsimd.memset(mask_q[:], 0.0)
            nc.gpsimd.memset(minus_half[:], -0.5).then_inc(ln_step, 1)
            pool.wait_ge(ln_step, 1)
            for ident in (ident16, ident32):
                nc.gpsimd.affine_select(ident[:], ident[:], [[-1, P]], ALU.not_equal, 1.0, base=0, channel_multiplier=1)
            nc.gpsimd.affine_select(mask_q[:], mask_q[:], [[-1, P]], ALU.is_ge, MASKED, base=0, channel_multiplier=1).then_inc(consts, 1)
            LN_STEPS = 9

            def normalise(b, first=False):
                mean, var = mean_var[:, :, 0], mean_var[:, :, 1]
                a1, r1, sq, v2, a2, r2, rr, shift = (ln[:, k, :] for k in range(8))

                def step(k, ins):
                    ins.then_inc(ln_step, 1)
                    pool.wait_ge(ln_step, b * LN_STEPS + 1 + k)
                    alone(pool)

                pool.wait_ge(mv_ready, b * NT + NT)
                if not first:
                    pool.wait_ge(v_ready, b * NT)
                    pool.wait_ge(rows_dma, b * 16)
                alone(pool)
                step(1, nc.gpsimd.tensor_scalar(a1, var, LN_EPS, None, ALU.add))
                step(2, nc.gpsimd.tensor_tensor(r1, a1, minus_half[:], ALU.pow))
                step(3, nc.gpsimd.tensor_tensor(sq, r1, r1, ALU.mult))
                step(4, nc.gpsimd.tensor_tensor(v2, sq, var, ALU.mult))
                step(5, nc.gpsimd.tensor_scalar(a2, v2, BIT_EPS, None, ALU.add))
                step(6, nc.gpsimd.tensor_tensor(r2, a2, minus_half[:], ALU.pow))
                step(7, nc.gpsimd.tensor_tensor(rr, r1, r2, ALU.mult))
                step(8, nc.gpsimd.tensor_tensor(shift, mean, rr, ALU.mult))
                step(9, nc.gpsimd.tensor_tensor(norm_c[:], a2, r2, ALU.mult))
                nc.gpsimd.tensor_scalar(shift, shift, -1.0, None, ALU.mult).then_inc(ln_ready, 1)

            def add_x(b):
                for t in range(NT):
                    pool.wait_ge(resid_dma[t % 2], b * 32 + 16 * (t // 2) + 16)
                    pool.wait_ge(scaled_ready, b * NT + t + 1)
                    nc.gpsimd.tensor_tensor(result[:, t, :], result[:, t, :], resid[:, t % 2, :], ALU.add).then_inc(result_ready, 1)

            def body(b, first=False, last=False):
                if first:
                    magnitudes_all(0)
                    for u in BELOW_BEFORE_ROPE:
                        below_threshold(u)
                for pair in range(4):
                    for half in range(2):
                        pool.wait_ge(rot_hi_ready, b * 8 + 2 * pair + half + 1)
                        nc.gpsimd.tensor_tensor(split_buf[:, pair % 2, 2 + half, :], rope_sum[:, pair % 2, half, :],
                                                split_buf[:, pair % 2, half, :], ALU.subtract).then_inc(rot_lo_ready, 1)
                    for u in BELOW_AFTER_ROPE[pair] if first else []:
                        if u == n_first + FC // 2:
                            magnitudes_all(1)
                        below_threshold(u)
                if not first:
                    add_x(b - 1)
                for f in range(1, FC):
                    pool.wait_ge(sq_ready, b * FC + f + 1)
                    if f >= 2:
                        pool.wait_ge(sq_added, b * (FC - 1) + f - 1)
                    nc.gpsimd.tensor_tensor(sq_sum[:], sq_sum[:], squares[:, f % 2, :], ALU.add).then_inc(sq_added, 1)
                if first:
                    largest_all(3, 3)
                pool.wait_ge(var_ready, b + 1)
                nc.gpsimd.tensor_tensor(ffn[:, 8, :], ffn[:, 5, :], minus_half[:], ALU.pow).then_inc(rstd_ready, 1)
                if not first and not last:
                    normalise(b + 1)

                def mask(g):
                    for k in range(GH):
                        pool.wait_ge(probs_ready, b * H + GH * g + k + 1)
                        alone(pool)
                        head = probs[:, g % 2, k, :]
                        for blocks in (head[:, 0:1024].rearrange("p (j c) -> p j c", c=512)[:, :, 0:P],
                                       head[:, KEY_COLS[3]:KEY_COLS[3] + 2 * P].rearrange("p (j c) -> p j c", c=P)):
                            nc.gpsimd.affine_select(blocks, blocks, [[0, 2], [1, P]], ALU.is_ge, 0.0, base=0,
                                                    channel_multiplier=-1).then_inc(probs_masked, 1)

                def split_context(g):
                    pool.wait_ge(ctx_ready, b * NG + g + 1)
                    alone(pool)
                    nc.gpsimd.tensor_copy(ctxT[:, 0, g, :], ctx_f32[:, g % 2, :]).then_inc(ctx_hi, 1)
                    pool.wait_ge(ctx_hi, b * NG + g + 1)
                    nc.gpsimd.tensor_tensor(ctxT[:, 1, g, :], ctx_f32[:, g % 2, :], ctxT[:, 0, g, :], ALU.subtract).then_inc(ctx_lo, 1)

                mask(0)
                mask(1)
                if first:
                    normalise(b + 1)
                mask(2)
                split_context(0)
                mask(3)
                for g in range(1, NG):
                    split_context(g)

            def largest_all(k, m):
                pool.wait_ge(w_max_ready, k + 1)
                nc.gpsimd.partition_all_reduce(col(m), w_all[:, m:m + 1], P, RMAX).then_inc(w_max_all, 1)

            def magnitudes_all(m):
                pool.wait_ge(w_abs_ready, m + 1)
                nc.gpsimd.partition_all_reduce(col(G_FC + m), w_all[:, 4 + m:5 + m], P, RADD).then_inc(w_abs_all, 1)
                pool.wait_ge(thresholds, m + 1)

            def below_threshold(u):
                k, m = u - n_first, int(units[u][0] == "proj")
                if k >= 4:
                    pool.wait_ge(w_unit_ready, u - 3)
                nc.gpsimd.tensor_scalar(below[:, (2 * k + 1) % 8, :], raw_parts(units[u])[1], col(MTHR + m), None,
                                        ALU.is_lt).then_inc(w_below_pool, 1)

            largest_all(0, 2)
            normalise(0, first=True)
            largest_all(1, 0)
            largest_all(2, 1)
            body(0, first=True)
            with pool.Fori(1, NB - 1) as b:
                body(b)
            body(NB - 1, last=True)
            add_x(NB - 1)


_INS = ["L0_attn_x", "L0_attn_Wq", "L0_attn_Wk", "L0_attn_Wv", "L0_attn_Wo", "L0_ffn_w_fc", "L0_ffn_w_proj"]


def rope_tables():
    import numpy as np

    inv_freq = np.exp(np.float32(-np.log(10000.0)) * np.arange(0, DK, 2, dtype=np.float32) / np.float32(DK))
    angle = np.arange(S, dtype=np.float32)[None, :] * np.repeat(inv_freq.astype(np.float32), HS)[:, None]
    return [np.ascontiguousarray(f(angle).astype(np.float32) * np.float32(ROPE_SHRINK)) for f in (np.cos, np.sin)]


def kernel(**inputs):
    import numpy as _np
    import concourse.bacc as _bacc
    from concourse import mybir as _mybir
    from concourse.bass_utils import run_bass_kernel_spmd as _run

    nc = _bacc.Bacc("TRN2", target_bir_lowering=False, num_devices=1)
    arrays, args = {}, []
    named = [(name, _np.ascontiguousarray(inputs[name])) for name in _INS]
    named += list(zip(("rope_cos", "rope_sin"), rope_tables()))
    for name, a in named:
        arrays[f"in_{name}_dram"] = a
        args.append(nc.dram_tensor(f"in_{name}_dram", a.shape, _mybir.dt.from_np(a.dtype), kind="ExternalInput").ap())
    args.append(nc.dram_tensor("out_0_dram", (NB, S, D), F32, kind="ExternalOutput").ap())
    args.append(nc.dram_tensor("norm_row", (S,), F32, kind="Internal").ap())
    program(nc, *args)
    r = _run(nc, [arrays], core_ids=[0])
    return r.results[0]["out_0_dram"]
```

```python
from contextlib import ExitStack

import concourse.bass as bass
from concourse import mybir

F32 = mybir.dt.float32
F16 = mybir.dt.float16
BF16 = mybir.dt.bfloat16
ALU = mybir.AluOpType
ACT = mybir.ActivationFunctionType
AX_X = mybir.AxisListType.X
RMAX = bass.bass_isa.ReduceOp.max
RADD = bass.bass_isa.ReduceOp.add

P = 128
NB, S, D = 8, 512, 512
H, DK = 16, 32
NF = DK // 2
F = 4 * D
NT = S // P
ND = D // P
FC = F // P
HS = P // NF
GH = P // DK
NG = H // GH
KS = 3 * DK
SPLITS = 3
KM = KS + SPLITS
INV_GROW = 4096.0
ROPE_SHRINK = 1.0 / 16
LN_EPS, BIT_EPS = 1e-5, 1e-6
MASKED = -1e30
KEY_COLS = [0, 512, 1024, 896]
PROBS = 1280
ROUNDS = [(i, h, S // ((i + 1) * P)) for i in (3, 2, 1, 0) for h in range(0, H, S // ((i + 1) * P))]
NR = len(ROUNDS)
S_BANKS = (2, 3, 4, 5, 1)
NSB = len(S_BANKS)
EARLY = 4
STATS_AFTER = (5, 7, 9, 11)
BIAS_DVE = 4
IN_BANK_1 = max(r for r in range(NR) if S_BANKS[r % NSB] == 1) + 1
N_LEFT = sum(i > 0 for i, _, _ in ROUNDS)
N_ABS = 8
ABS_ACT = 4
DOWN_MATMULS = 2 * FC
DOWN_BESIDE_SCORES = (NT - 1) * DOWN_MATMULS
EXP_COLS = [sum(n * ((i + 1) * P + 300) for i, _, n in ROUNDS[:r + 1]) for r in range(NR)]
DOWN_AFTER_ROUND = [DOWN_BESIDE_SCORES * c // EXP_COLS[-1] for c in EXP_COLS]
KEEP_DOWN = tuple(1 + min(r for r in range(NR) if DOWN_AFTER_ROUND[r] >= (t + 1) * DOWN_MATMULS) for t in range(2))
DOWN_BESIDE_EXP = 12
DOWN_PER_HEAD = 4
DOWN_BEFORE_MAXIMA = DOWN_BESIDE_SCORES + 8
X_BANKS = (3, 4, 5, 2)


def program(nc, x, w_q, w_k, w_v, w_o, w_fc, w_proj, rope_cos, rope_sin, out, norm_row):
    with ExitStack() as ctx:
        def sb(name, shape, dt):
            return ctx.enter_context(nc.sbuf_tensor(name, shape, dt))

        def sem(name):
            return ctx.enter_context(nc.semaphore(name))

        qkT = sb("qkT", [P, 2, 2, ND, 2, 2, P], F16)
        voT = sb("voT", [P, 2, 2, ND, D], F16)
        fcT = sb("fcT", [P, ND, F], F16)
        projT = sb("projT", [P, FC, D], F16)
        stacks = sb("stacks", [P, 2, H, S], F16)
        q_stack, k_stack = stacks[:, 0], stacks[:, 1]
        arena = sb("arena", [P, 2, GH, PROBS], F32)
        probs = arena[:]
        arena_f = arena[:].rearrange("p a b c -> p (a b c)")
        hid = arena_f[:, 0:8192].bitcast(F16).rearrange("p (s f t) -> p s f t", s=2, f=FC)
        rope_prods = arena_f[:, 8192:10240].rearrange("p (k t) -> p k t", k=4)
        result = rope_prods
        xr_buf = sb("xr_buf", [P, NT, D], F32)
        x_sb = xr_buf[:]
        rope_sum = xr_buf[:].rearrange("p (a b) t -> p a b t", a=2)
        xh_buf = sb("xh_buf", [P, NT, D], F32)
        xhat = xh_buf[:]
        gelu_out = xh_buf[:]
        xT = sb("xT", [P, 2, ND, S], F16)
        rope_tab = sb("rope_tab", [P, 2, S], F32)
        mix = sb("mix", [P, 2, S], F32)
        rope_row = mix[:]
        norm_rows = mix[:, 0, :]
        tanh_sb = xr_buf[:]
        row_max = mix[:, 0, 0:NT * H].rearrange("p (i h) -> p i h", i=NT)
        max_parts = mix[:, 0, 64:160].bitcast(F16).rearrange("p (i s h) -> p i s h", i=NT, s=SPLITS)
        exp_bias = mix[:, 0, 160:224].rearrange("p (i h) -> p i h", i=NT)
        part_rest = mix[:, 0, 224:288].rearrange("p (i h) -> p i h", i=NT)
        left_max = mix[:, 0, 288:352].rearrange("p (i h) -> p i h", i=NT)
        row_sum = mix[:, 0, 352:416].rearrange("p (i h) -> p i h", i=NT)
        inv_parts = mix[:, 0, 416:512].bitcast(F16).rearrange("p (i s h) -> p i s h", i=NT, s=SPLITS)
        bn = mix[:, 0, 64:64 + 6 * NT].rearrange("p (t k) -> p t k", t=NT)
        maxT = mix[0:SPLITS * H, 1, 0:S // 2].bitcast(F16)
        split_buf = sb("split_buf", [P, 2, 4, S], F16)
        split_f = split_buf[:].rearrange("p a b t -> p (a b t)").bitcast(F32)
        squares = split_f[:, 0:1024].rearrange("p (a t) -> p a t", a=2)
        ctx_f32 = split_f[:, 0:1024].rearrange("p (a t) -> p a t", a=2)
        inv_spread = split_f[:, 1024:1536]
        invT = split_f[0:SPLITS * H, 1536:1536 + S // 2].bitcast(F16)
        sq_sum = split_f[:, 1536:2048]
        v_sb = sb("v_sb", [P, NT, D], F32)
        ctxT = sb("ctxT", [P, 2, NG, S], F16)
        gate = sb("gate", [P, NT, D], F32)
        resid = sb("resid", [P, 2, D], F32)
        w_rowsum = sb("w_rowsum", [P, D], F16)
        ident16 = sb("ident16", [P, P], F16)
        ident32 = sb("ident32", [P, P], F32)
        mask_q = sb("mask_q", [P, P], BF16)
        selector = sb("selector", [SPLITS * H, H, DK], F16)
        ones32 = sb("ones32", [P, 1], F32)
        ones16 = sb("ones16", [P, P], F16)
        mean_var = sb("mean_var", [P, NT, 2], F32)
        ln = sb("ln", [P, 8, NT], F32)
        norm_c = sb("norm_c", [P, NT], F32)
        minus_half = sb("minus_half", [P, NT], F32)
        ffn = sb("ffn", [P, 12, NT], F32)
        gate_scale = sb("gate_scale", [P, 2, NT], F32)
        w_part = ffn[:].rearrange("p k t -> p (k t)")[:, 0:2 * N_ABS]
        w_all = sb("w_all", [P, 6], F32)
        scl = sb("scl", [P, 20], F32)

        raw_attn = [gate[:], ctxT[:].rearrange("p a b t -> p (a b t)").bitcast(F32).rearrange("p (a t) -> p a t", a=ND),
                    v_sb[:], x_sb]
        raw_fc = stacks[:].rearrange("p a h t -> p (a h t)").bitcast(F32).rearrange("p (c d) -> p c d", c=FC)
        raw_proj = arena_f[:, 0:8192].rearrange("p (c d) -> p c d", c=ND)
        rings = [split_buf[:].rearrange("p a (b s) t -> p (a b) s t", s=2), ctxT[:].rearrange("p a (b s) t -> p (a b) s t", s=2)]
        below = gate[:].rearrange("p a t -> p (a t)").bitcast(F16).rearrange("p (a t) -> p a t", a=8)
        magnitudes = resid[:].rearrange("p a t -> p (a t)")

        banks = ctx.enter_context(nc.psum_tensor("banks", [P, 8, 512], F32))
        banks16 = banks[:].rearrange("p b c -> p (b c)").bitcast(F16).rearrange("p (b c) -> p b c", b=8)
        st_region = [banks[:, 0:3, :].rearrange("p b c -> p (b c)"), banks[:, 3:6, :].rearrange("p b c -> p (b c)")]

        w_dma = [sem(f"w_dma{i}") for i in range(6)]
        tab_dma, ones_dma = sem("tab_dma"), sem("ones_dma")
        stood_alone = sem("stood_alone")
        consts = sem("consts")
        w_max_ready, w_max_all = sem("w_max_ready"), sem("w_max_all")
        w_abs_part, w_abs_dve, w_abs_ready, w_abs_all = sem("w_abs_part"), sem("w_abs_dve"), sem("w_abs_ready"), sem("w_abs_all")
        attn_scl_step, ffn_scl_step = sem("attn_scl_step"), sem("ffn_scl_step")
        w_hi_ready, w_unit_ready = sem("w_hi_ready"), sem("w_unit_ready")
        w_below_pool, w_below_dve = sem("w_below_pool"), sem("w_below_dve")
        w_turned, w_kept = sem("w_turned"), sem("w_kept")
        thresholds = sem("thresholds")
        rowsum_ps, rowsum_kept = sem("rowsum_ps"), sem("rowsum_kept")
        x_dma, out_dma, max_dma = sem("x_dma"), sem("out_dma"), sem("max_dma")
        resid_dma = [sem("resid_dma0"), sem("resid_dma1")]
        stack_dma = [sem("stack_dma0"), sem("stack_dma1")]
        bn_ready, mv_ready, ln_step = sem("bn_ready"), sem("mv_ready"), sem("ln_step")
        xhat_ready, row_dma, rows_dma = sem("xhat_ready"), sem("row_dma"), sem("rows_dma")
        xT_ps, xhi_ready, xlo_ready = sem("xT_ps"), sem("xhi_ready"), sem("xlo_ready")
        rope_row_ready = sem("rope_row_ready")
        qk_ps, rope_prod_ready, rope_sum_ready = sem("qk_ps"), sem("rope_prod_ready"), sem("rope_sum_ready")
        rot_hi_ready, rot_lo_ready = sem("rot_hi_ready"), sem("rot_lo_ready")
        v_ps, v_ready = sem("v_ps"), sem("v_ready")
        wo_ps, scaled_ready, result_ready = sem("wo_ps"), sem("scaled_ready"), sem("result_ready")
        fc_ps, gelu_ready = sem("fc_ps"), sem("gelu_ready")
        hid_hi_ready, hid_lo_ready = sem("hid_hi_ready"), sem("hid_lo_ready")
        sq_ready, sq_added, sq_ps = sem("sq_ready"), sem("sq_added"), sem("sq_ps")
        down_ps, down_kept = sem("down_ps"), sem("down_kept")
        s_ps, left_ready, max_ready = sem("s_ps"), sem("left_ready"), sem("max_ready")
        exp_bias_dve, exp_bias_ready, sum_ready = sem("exp_bias_dve"), sem("exp_bias_ready"), sem("sum_ready")
        max_step, max_split, inv_ready, inv_step, inv_split = sem("max_step"), sem("max_split"), sem("inv_ready"), sem("inv_step"), sem("inv_split")
        invT_ps, invT_ready = sem("invT_ps"), sem("invT_ready")
        selector_step = sem("selector_step")
        maxT_ps, maxT_ready = sem("maxT_ps"), sem("maxT_ready")
        sums_read, ffn_step, var_ready, rstd_ready = sem("sums_read"), sem("ffn_step"), sem("var_ready"), sem("rstd_ready")
        ln_ready = sem("ln_ready")
        centred, tanh_ready, gate_ready = sem("centred"), sem("tanh_ready"), sem("gate_ready")
        st_ps, probs_ready, probs_masked, pv_ps = sem("st_ps"), sem("probs_ready"), sem("probs_masked"), sem("pv_ps")
        spread_ps, spread_kept, ctx_ready = sem("spread_ps"), sem("spread_kept"), sem("ctx_ready")
        ctx_hi, ctx_lo = sem("ctx_hi"), sem("ctx_lo")

        S_Q, S_K, S_V, S_O, INV, EXP_SCALE, SVO = 0, 1, 2, 3, 4, 8, 9
        G_FC, G_PROJ, INV_G, THR, MTHR, BIT_EPS_G, HALF_GP = 10, 11, 12, 13, 15, 17, 18

        def col(c):
            return scl[:, c:c + 1]

        units = [("attn", m, o) for m in (2, 0, 1) for o in range(ND)]
        n_first = len(units)
        units += [("fc", o) for o in range(0, FC, 2)]
        units += [("proj", o, f) for o in range(ND) for f in range(0, 4, 2)]
        n_tern = len(units) - n_first
        units += [("attn", 3, o) for o in range(ND)]
        n_units = len(units)
        fu = [n_first + k for k in range(n_tern)]
        TURNS_AFTER_V = [[], [], [], fu[0:2]]
        TURNS_AFTER_QK = [fu[2:4], fu[4:5], fu[5:6], fu[6:8], [], fu[8:10], [], fu[10:12]]
        TURNS_IN_UP = fu[12:16]
        MADE_BEFORE_ROPE = fu[0:6]
        MADE_AFTER_ROPE = [fu[6:8], fu[8:10], fu[10:12], fu[12:16]]
        BELOW_BEFORE_ROPE = fu[0:8]
        BELOW_AFTER_ROPE = [fu[8:10], fu[10:12], fu[12:14], fu[14:16]]

        def turn_bank(u):
            if u < n_first:
                return (6, 7, 0, 1)[u % 4]
            return 6 + u % 2 if u < n_first + n_tern else 2 + u % 4

        def ring(u):
            return rings[u >= n_first][:, u % 4]

        def raw_parts(unit):
            if unit[0] == "fc":
                return [raw_fc[:, unit[1] + k, :] for k in range(2)]
            return [raw_proj[:, unit[1], (unit[2] + k) * 512:(unit[2] + k + 1) * 512] for k in range(2)]

        block = ctx.enter_context(nc.Block())

        def alone(eng):
            eng.sem_inc(stood_alone, 1)

        @block.sync
        def _(sp):
            def load_weight(raw, w, n):
                sp.dma_start(raw, w.rearrange("(c p) d -> p c d", p=P)).then_inc(w_dma[n], 16)

            load_weight(raw_attn[2], w_v, 2)
            sp.dma_start(x_sb, x[0].rearrange("(t p) d -> p t d", p=P)).then_inc(x_dma, 16)
            load_weight(raw_attn[0], w_q, 0)
            load_weight(raw_attn[1], w_k, 1)
            sp.dma_start(rope_tab[:, 0, :], rope_cos).then_inc(tab_dma, 16)
            sp.dma_start(rope_tab[:, 1, :], rope_sin).then_inc(tab_dma, 16)
            load_weight(raw_fc, w_fc, 4)
            load_weight(raw_proj, w_proj, 5)

            def load_resid(b, t):
                if t >= 2:
                    sp.wait_ge(result_ready, b * NT + t - 1)
                sp.dma_start(resid[:, t % 2, :], x[b].rearrange("(t p) d -> t p d", p=P)[t]).then_inc(resid_dma[t % 2], 16)

            def store_result(b):
                for t in range(NT):
                    sp.wait_ge(result_ready, b * NT + t + 1)
                    sp.dma_start(out[b].rearrange("(t p) d -> t p d", p=P)[t], result[:, t, :]).then_inc(out_dma, 16)
                    if t + 2 < NT:
                        load_resid(b, t + 2)

            def spread_norms(b, first=False):
                sp.wait_ge(ln_ready, b + 1)
                for t in range(NT):
                    sp.dma_start(norm_row[t * P:(t + 1) * P], norm_c[:, t:t + 1]).then_inc(row_dma, 16)
                sp.wait_ge(row_dma, b * NT * 16 + NT * 16)
                if not first:
                    sp.wait_ge(invT_ready, b)
                sp.dma_start(norm_rows, norm_row.partition_broadcast(P)).then_inc(rows_dma, 16)

            def body(b, first=False, last=False):
                if not first:
                    load_resid(b - 1, 0)
                    load_resid(b - 1, 1)
                else:
                    sp.wait_ge(w_kept, n_first + FC // 2)
                    for row in range(KS, KM):
                        sp.dma_start(k_stack[row:row + 1, :, :], ones16[0:H * S // P, :]).then_inc(ones_dma, 16)
                for pair in range(4):
                    stack, heads = (q_stack, k_stack)[pair // 2], slice(HS * (pair % 2), HS * (pair % 2 + 1))
                    if pair == 0 and not first:
                        sp.wait_ge(st_ps, b * H)
                    sp.wait_ge(rot_lo_ready, b * 8 + 2 * pair + 2)
                    order = ((0, 0, 1), (0, 1, 0))[pair // 2]
                    for third, part in enumerate(order):
                        for half in range(2):
                            row = third * DK + half * NF
                            sp.dma_start(stack[row:row + NF, heads, :], split_buf[:, pair % 2, 2 * part + half, :]
                                         ).then_inc(stack_dma[pair % 2], 16)

                def load_next():
                    sp.dma_start(x_sb, x[b + 1].rearrange("(t p) d -> p t d", p=P)).then_inc(x_dma, 16)

                if first:
                    load_weight(raw_attn[3], w_o, 3)
                elif not last:
                    load_next()
                if not first:
                    store_result(b - 1)
                sp.wait_ge(maxT_ready, b + 1)
                sp.dma_start(q_stack[KS:KM, :, :], maxT[:, :]).then_inc(max_dma, 16)
                if first:
                    sp.wait_ge(w_unit_ready, n_units)
                    load_next()
                if not last:
                    spread_norms(b + 1)

            spread_norms(0, first=True)
            body(0, first=True)
            with sp.Fori(1, NB - 1) as b:
                body(b)
            body(NB - 1, last=True)
            load_resid(NB - 1, 0)
            load_resid(NB - 1, 1)
            store_result(NB - 1)
            sp.wait_ge(out_dma, NB * NT * 16)

        @block.tensor
        def _(pe):
            pe.wait_ge(consts, 1)

            def turn_weights(first, end):
                for u in range(first, end):
                    pe.wait_ge(w_unit_ready, u + 1)
                    if u < n_first and u >= 4:
                        pe.wait_ge(w_kept, u - 3)
                    if n_first + 2 <= u < n_first + n_tern:
                        pe.wait_ge(w_kept, u - 1)
                    for k in range(8):
                        mm = pe.transpose(banks16[:, turn_bank(u), k * P:(k + 1) * P],
                                          ring(u)[:, k // 4, (k % 4) * P:(k % 4 + 1) * P], ident16[:])
                    mm.then_inc(w_turned, 1)

            def ternary_row_sums():
                pe.wait_ge(w_kept, n_first + n_tern)
                for f in range(FC):
                    mm = pe.matmul(banks[:, 7, :], ones16[:], projT[:, f, :], start=(f == 0), stop=(f == FC - 1))
                mm.then_inc(rowsum_ps, 1)

            def three_products(out_ap, hi_lo, n, key):
                for c in range(n):
                    for k, (a, r) in enumerate(((0, 0), (0, 1), (1, 0))):
                        lhs, rhs = hi_lo(a, r, c)
                        mm = pe.matmul(out_ap, lhs, rhs, start=(c == 0 and k == 0), stop=(c == n - 1 and k == 2))
                return mm

            def out_projection(b):
                for t in range(NT):
                    if t == 0:
                        pe.wait_ge(ctx_lo, b * NG + NG)
                    if t >= 2:
                        pe.wait_ge(scaled_ready, b * NT + t - 1)
                    three_products(banks[:, 6 + t % 2, :],
                                   lambda a, r, c: (ctxT[:, a, c, t * P:(t + 1) * P], voT[:, 1, r, c, :]),
                                   NG, "o").then_inc(wo_ps, 1)

            def turn_tokens(b, t, first=False):
                if t == 0 and not first:
                    pe.wait_ge(probs_ready, b * H - 1)
                if t == 3 and not first:
                    pe.wait_ge(probs_ready, b * H)
                pe.wait_ge(xhat_ready, b * NT + t + 1)
                for c in range(ND):
                    mm = pe.transpose(banks[:, X_BANKS[t], c * P:(c + 1) * P], xhat[:, t, c * P:(c + 1) * P], ident32[:])
                mm.then_inc(xT_ps, 1)

            def last_out_projection(b):
                for last in (0, 1):
                    pe.wait_ge(ctx_lo, b * NG + NG - 1 + last)
                    for t in range(NT):
                        for c in (range(NG - 1), range(NG - 1, NG))[last]:
                            for k, (a, r) in enumerate(((0, 0), (0, 1), (1, 0))):
                                mm = pe.matmul(banks[:, t, :], ctxT[:, a, c, t * P:(t + 1) * P], voT[:, 1, r, c, :],
                                               start=(c == 0 and k == 0), stop=(c == NG - 1 and k == 2))
                        if last:
                            mm.then_inc(wo_ps, 1)

            def body(b, first=False, last=False):
                for t in range(NT):
                    pe.wait_ge(xlo_ready, b * NT + t + 1)
                    if t == 0 and first:
                        pe.wait_ge(w_kept, n_first)
                    if t >= 2:
                        pe.wait_ge(v_ready, b * NT + t - 1)
                    three_products(banks[:, t % 2, :],
                                   lambda a, r, c: (xT[:, a, c, t * P:(t + 1) * P], voT[:, 0, r, c, :]),
                                   ND, "v").then_inc(v_ps, 1)
                    for u in TURNS_AFTER_V[t] if first else []:
                        turn_weights(u, u + 1)
                for pair in range(4):
                    if pair >= 2:
                        pe.wait_ge(rope_prod_ready, b * 16 + 4 * (pair - 2) + 4)
                    for half in range(2):
                        three_products(banks[:, 2 + 2 * (pair % 2) + half, :],
                                       lambda a, r, c: (qkT[:, pair // 2, r, c, pair % 2, half, :], xT[:, a, c, :]),
                                       ND, "qk").then_inc(qk_ps, 1)
                        for u in TURNS_AFTER_QK[2 * pair + half] if first else []:
                            turn_weights(u, u + 1)
                if not first:
                    out_projection(b - 1)
                def score_round(r):
                    i, h0, n = ROUNDS[r]
                    if r == 0:
                        for s in stack_dma:
                            pe.wait_ge(s, (b + 1) * 192)
                        pe.wait_ge(rope_prod_ready, b * 16 + 16)
                    if r >= NSB:
                        pe.wait_ge(sum_ready, b * NR + r - NSB + 1)
                    keys = (i + 1) * P
                    for k in range(n):
                        mm = pe.matmul(banks[:, S_BANKS[r % NSB], k * keys:(k + 1) * keys], q_stack[0:KS, h0 + k, i * P:(i + 1) * P],
                                       k_stack[0:KS, h0 + k, 0:keys], start=True, stop=True)
                    mm.then_inc(s_ps, 1)

                for f in range(FC):
                    if f < 2:
                        pe.wait_ge(v_ready, b * NT + 3 + f)
                    else:
                        pe.wait_ge(gelu_ready, b * FC + f - 1)
                    for c in range(ND):
                        for part in range(2):
                            mm = pe.matmul(banks[:, f % 2, :], fcT[:, c, f * P:(f + 1) * P], xT[:, part, c, :],
                                           start=(c == 0 and part == 0), stop=(c == ND - 1 and part == 1))
                    mm.then_inc(fc_ps, 1)
                    for u in TURNS_IN_UP if first and f == 1 else []:
                        turn_weights(u, u + 1)
                    if f >= FC - EARLY:
                        score_round(f - (FC - EARLY))

                def down():
                    for t in range(NT):
                        if t == 0:
                            if not first:
                                pe.wait_ge(scaled_ready, b * NT)
                            pe.wait_ge(gelu_ready, b * FC + FC)
                        if t == 1 and first:
                            pe.wait_ge(rowsum_kept, 1)
                        if t >= 2:
                            pe.wait_ge(down_kept, b * 2 + t - 1)
                        order = [(f, part) for f in range(FC) for part in range(2)]
                        if t == NT - 1:
                            order = [(f, part) for part in range(2) for f in range(FC)]
                        for f, part in order:
                            if t == 0 and part == 0:
                                pe.wait_ge(hid_lo_ready, b * FC + f + 1)
                            lhs = hid[:, part, f, t * P:(t + 1) * P]
                            ends = dict(start=(f == 0 and part == 0), stop=(f == FC - 1 and part == 1))
                            if t < NT - 1:
                                pe.matmul(banks[:, 0, t:t + 1], lhs, ones16[:, 0:1], **ends)
                            mm = pe.matmul(banks[:, 6 + t % 2, :], lhs, projT[:, f, :], **ends)
                            if ends["stop"]:
                                mm.then_inc(down_ps, 1)
                            yield

                if first:
                    ternary_row_sums()
                downs = down()
                given = 0
                for r in range(NR):
                    if r >= EARLY:
                        score_round(r)
                    while given < DOWN_AFTER_ROUND[r]:
                        next(downs)
                        given += 1
                while given < DOWN_BEFORE_MAXIMA:
                    next(downs)
                    given += 1
                pe.wait_ge(max_split, b + 1)
                alone(pe)
                pe.wait_ge(sum_ready, b * NR + IN_BANK_1)
                alone(pe)
                for i in range(NT):
                    mm = pe.transpose(banks16[0:SPLITS * H, 1, i * P:(i + 1) * P],
                                      max_parts[:, i].rearrange("p s h -> p (s h)"), ident16[:])
                mm.then_inc(maxT_ps, 1)
                for f in range(FC):
                    for part in range(2):
                        pe.matmul(banks[:, 0, NT - 1:NT], hid[:, part, f, S - P:S], ones16[:, 0:1],
                                  start=(f == 0 and part == 0), stop=(f == FC - 1 and part == 1))
                pe.wait_ge(sq_added, b * (FC - 1) + FC - 1)
                for t in range(NT):
                    mm = pe.matmul(banks[:, 0, NT + t:NT + t + 1], sq_sum[:, t * P:(t + 1) * P], ones32[:], start=True, stop=True)
                mm.then_inc(sq_ps, 1)
                while given < NT * DOWN_MATMULS - DOWN_BESIDE_EXP:
                    next(downs)
                    given += 1

                pe.wait_ge(sum_ready, b * NR + NR)
                if first:
                    turn_weights(n_first + n_tern, n_units)
                def scores(h):
                    if h == 0 and first:
                        pe.wait_ge(w_kept, n_units)
                        pe.wait_ge(ones_dma, 16 * SPLITS)
                    if h == 0:
                        pe.wait_ge(max_dma, (b + 1) * 16)
                    if h == 1:
                        pe.wait_ge(sums_read, b + 1)
                    if h >= 2:
                        pe.wait_ge(probs_ready, b * H + h - 1)
                    ps = st_region[(h + 1) % 2]
                    for j in (0, 1, 3, 2):
                        at, n = KEY_COLS[j], S - j * P
                        mm = pe.matmul(ps[:, at:at + n], k_stack[0:KM, h, j * P:(j + 1) * P], q_stack[0:KM, h, j * P:S],
                                       start=True, stop=True)
                    mm.then_inc(st_ps, 1)

                def turn_inverses():
                    pe.wait_ge(inv_split, b + 1)
                    alone(pe)
                    pe.wait_ge(centred, b * NT + NT - 1)
                    alone(pe)
                    for i in range(NT):
                        mm = pe.transpose(banks16[0:SPLITS * H, 6, i * P:(i + 1) * P],
                                          inv_parts[:, i].rearrange("p s h -> p (s h)"), ident16[:])
                    mm.then_inc(invT_ps, 1)

                def weigh(g, j):
                    if j == 0:
                        pe.wait_ge(probs_masked, 2 * (b * H + GH * (g + 1)) - 1)
                    if j == 2:
                        pe.wait_ge(probs_masked, 2 * (b * H + GH * (g + 1)))
                    if j == 0:
                        if g == 0:
                            pe.wait_ge(invT_ready, b + 1)
                        else:
                            pe.wait_ge(ctx_ready, b * NG + g)
                    if j == 1:
                        if g == 0:
                            pe.wait_ge(centred, b * NT + NT)
                        pe.matmul(banks[:, 7, :], selector[:, GH * g:GH * (g + 1), :].rearrange("p h d -> p (h d)"), invT,
                                  start=True, stop=True).then_inc(spread_ps, 1)
                    at, n = KEY_COLS[j], S - j * P
                    for k in range(GH):
                        head = GH * g + k
                        mm = pe.matmul(banks[k * DK:(k + 1) * DK, 6, j * P:S], v_sb[:, j, head * DK:(head + 1) * DK],
                                       probs[:, g % 2, k, at:at + n], start=(j == 0), stop=(j == NT - 1),
                                       tile_position=(0, k * DK))
                    if j == NT - 1:
                        mm.then_inc(pv_ps, 1)

                for g in range(NG + 1):
                    for k in range(GH):
                        if g < NG:
                            scores(GH * g + k)
                        for _ in range(DOWN_PER_HEAD if g == 0 else 0):
                            next(downs, None)
                        if g == 0 and k == GH - 1:
                            turn_inverses()
                        if g > 0 and k > 0:
                            weigh(g - 1, k - 1)
                        if g == NG and not last:
                            if k == 0:
                                for t in range(3):
                                    turn_tokens(b + 1, t)
                            if k == 1:
                                turn_tokens(b + 1, 3)
                    if g > 0:
                        weigh(g - 1, NT - 1)

            turn_weights(0, ND)
            for t in range(NT):
                turn_tokens(0, t, first=True)
            turn_weights(ND, n_first)
            body(0, first=True)
            with pe.Fori(1, NB - 1) as b:
                body(b)
            body(NB - 1, last=True)
            last_out_projection(NB - 1)

        @block.scalar
        def _(act):
            def keep_weights(u):
                unit = units[u]
                act.wait_ge(w_turned, u + 1)
                src = banks16[:, turn_bank(u), :]
                if unit[0] == "fc":
                    dst = fcT[:, :, unit[1] * P:(unit[1] + 2) * P].rearrange("p c (o n) -> p o c n", o=2)
                    mm = nc.scalar.copy(dst, src.rearrange("p (o c n) -> p o c n", o=2, c=ND))
                elif unit[0] == "proj":
                    _, o, f = unit
                    mm = nc.scalar.copy(projT[:, 4 * f:4 * f + 8, o * P:(o + 1) * P], src.rearrange("p (f n) -> p f n", f=8))
                else:
                    _, m, o = unit
                    src = src.rearrange("p (s c n) -> p s c n", s=2, c=ND)
                    if m >= 2:
                        mm = nc.scalar.copy(voT[:, m - 2, :, :, o * P:(o + 1) * P], src)
                    for part, half in [(p, h) for p in range(2) for h in range(2)] if m < 2 else []:
                        part_src = src[:, part].rearrange("p c (h f two) -> p c f h two", h=GH, two=2)[:, :, :, :, half]
                        dst = qkT[:, m, part, :, o // 2, half, :].rearrange("p c (f h) -> p c f h", h=HS)
                        mm = nc.scalar.copy(dst[:, :, :, GH * (o % 2):GH * (o % 2) + GH], part_src)
                mm.then_inc(w_kept, 1)

            def sum_magnitudes(m, k):
                raw = (raw_fc, raw_proj)[m].rearrange("p c d -> p (c d)")
                width = F * D // P // N_ABS
                act.wait_ge(w_dma[4 + m], 16)
                if m or k:
                    act.wait_ge(w_abs_part, ABS_ACT * m + k)
                nc.scalar.activation(magnitudes, raw[:, k * width:(k + 1) * width], ACT.Abs,
                                     accum_out=w_part[:, N_ABS * m + k:N_ABS * m + k + 1]).then_inc(w_abs_part, 1)

            def normalise(b, t):
                act.wait_ge(ln_ready, b + 1)
                nc.scalar.activation(xhat[:, t, :], x_sb[:, t, :], ACT.Identity, scale=ln[:, 6, t:t + 1],
                                     bias=ln[:, 7, t:t + 1]).then_inc(xhat_ready, 1)

            def split_tokens(b):
                for t in range(NT):
                    act.wait_ge(xT_ps, b * NT + t + 1)
                    nc.scalar.copy(xT[:, 0, :, t * P:(t + 1) * P],
                                   banks[:, X_BANKS[t], :].rearrange("p (c n) -> p c n", c=ND)).then_inc(xhi_ready, 1)

            for u in range(n_first):
                keep_weights(u)
                if u == ND - 1:
                    for t in range(NT):
                        normalise(0, t)
            split_tokens(0)
            for k in range(ABS_ACT):
                sum_magnitudes(0, k)

            def body(b, first=False, last=False):
                for t in range(NT):
                    act.wait_ge(v_ps, b * NT + t + 1)
                    nc.scalar.activation(v_sb[:, t, :], banks[:, t % 2, :], ACT.Copy, scale=norm_c[:, t:t + 1]).then_inc(v_ready, 1)
                    if first:
                        sum_magnitudes(1, t)
                for k, u in enumerate(MADE_BEFORE_ROPE if first else []):
                    keep_weights(u)
                    if NT + k < N_ABS:
                        sum_magnitudes(1, NT + k)

                for pair in range(4):
                    for half in range(2):
                        act.wait_ge(rope_sum_ready, b * 8 + 2 * pair + half + 1)
                        if half == 0 and pair >= 2:
                            act.wait_ge(stack_dma[pair % 2], b * 192 + 96)
                        if half == 0 and pair == 0 and not first:
                            act.wait_ge(ctx_lo, b * NG)
                        nc.scalar.copy(split_buf[:, pair % 2, half, :], rope_sum[:, pair % 2, half, :]).then_inc(rot_hi_ready, 1)
                    for u in MADE_AFTER_ROPE[pair] if first and pair < 3 else []:
                        keep_weights(u)

                nc.scalar.preload_act_table(ACT.Gelu)

                def square(f):
                    act.wait_ge(gelu_ready, b * FC + f + 1)
                    if f == 0:
                        for s in stack_dma:
                            act.wait_ge(s, (b + 1) * 192)
                    if f >= 3:
                        act.wait_ge(sq_added, b * (FC - 1) + f - 2)
                    dst = sq_sum[:] if f == 0 else squares[:, f % 2, :]
                    nc.scalar.activation(dst, gelu_out[:, f % 4, :], ACT.Square, scale=col(INV_G)).then_inc(sq_ready, 1)

                for f in range(FC):
                    act.wait_ge(fc_ps, b * FC + f + 1)
                    if f >= 4:
                        act.wait_ge(hid_lo_ready, b * FC + f - 3)
                        act.wait_ge(sq_ready, b * FC + f - 3)
                    nc.scalar.activation(gelu_out[:, f % 4, :], banks[:, f % 2, :], ACT.Gelu, scale=col(G_FC)).then_inc(gelu_ready, 1)
                    for u in TURNS_IN_UP if first and f == 0 else []:
                        keep_weights(u)
                    if f >= 1:
                        square(f - 1)
                nc.scalar.preload_act_table(ACT.Exp)
                square(FC - 1)
                if first:
                    act.wait_ge(rowsum_ps, 1)
                    nc.scalar.copy(w_rowsum[:], banks[:, 7, :]).then_inc(rowsum_kept, 1)
                for r, (i, h0, n) in enumerate(ROUNDS):
                    if r < BIAS_DVE:
                        act.wait_ge(exp_bias_dve, b * BIAS_DVE + r + 1)
                    else:
                        act.wait_ge(exp_bias_ready, b * (NR - BIAS_DVE) + r - BIAS_DVE + 1)
                    keys = (i + 1) * P
                    for k in range(n):
                        block = banks[:, S_BANKS[r % NSB], k * keys:(k + 1) * keys]
                        mm = nc.scalar.activation(block, block, ACT.Exp, scale=col(EXP_SCALE), bias=exp_bias[:, i, h0 + k:h0 + k + 1],
                                                  accum_out=row_sum[:, i, h0 + k:h0 + k + 1])
                    mm.then_inc(sum_ready, 1)
                    if r in KEEP_DOWN:
                        t = KEEP_DOWN.index(r)
                        act.wait_ge(down_ps, b * NT + t + 1)
                        nc.scalar.copy(gate[:, t, :], banks[:, 6 + t % 2, :]).then_inc(down_kept, 1)

                for u in range(n_first + n_tern, n_units) if first else []:
                    keep_weights(u)
                def split_context(g):
                    act.wait_ge(ctx_ready, b * NG + g + 1)
                    nc.scalar.copy(ctxT[:, 0, g, :], ctx_f32[:, g % 2, :]).then_inc(ctx_hi, 1)

                for h in range(H):
                    g = h // GH
                    act.wait_ge(st_ps, b * H + h + 1)
                    if h % GH == 0 and g == 1 and not first:
                        act.wait_ge(out_dma, b * NT * 16)
                    if h % GH == 0 and g >= 2:
                        act.wait_ge(pv_ps, b * NG + g - 1)
                    nc.scalar.activation(probs[:, g % 2, h % GH, :], st_region[(h + 1) % 2][:, 0:PROBS], ACT.Exp,
                                         scale=col(EXP_SCALE)).then_inc(probs_ready, 1)
                    if h % GH == 0 and g >= 2:
                        split_context(g - 2)
                if not last:
                    split_tokens(b + 1)
                split_context(2)
                for t in range(NT):
                    act.wait_ge(centred, b * NT + NT)
                    nc.scalar.activation(tanh_sb[:, t, :], gate[:, t, :], ACT.Tanh,
                                         scale=gate_scale[:, 0, t:t + 1]).then_inc(tanh_ready, 1)
                split_context(3)

            body(0, first=True)
            with act.Fori(1, NB - 1) as b:
                body(b)
            body(NB - 1, last=True)

        @block.vector
        def _(dve):
            def largest(m):
                dve.wait_ge(w_dma[m], 16)
                nc.vector.tensor_reduce(w_all[:, m:m + 1], raw_attn[m].rearrange("p c d -> p (c d)"), AX_X, ALU.max,
                                        apply_absolute_value=True).then_inc(w_max_ready, 1)

            def attn_step(k, ins):
                ins.then_inc(attn_scl_step, 1)
                dve.wait_ge(attn_scl_step, k)

            def split_weights(u):
                _, m, o = units[u]
                if 4 <= u:
                    dve.wait_ge(w_turned, u - 3)
                nc.vector.tensor_scalar(ring(u)[:, 0, :], raw_attn[m][:, o, :], col(INV + m), None, ALU.mult).then_inc(w_hi_ready, 1)
                dve.wait_ge(w_hi_ready, u + 1 if u < n_first else u + 1 - n_tern)
                nc.vector.scalar_tensor_tensor(ring(u)[:, 1, :], raw_attn[m][:, o, :], col(INV + m), ring(u)[:, 0, :],
                                               ALU.mult, ALU.subtract).then_inc(w_unit_ready, 1)

            def ffn_scales(m):
                def step(k, ins):
                    ins.then_inc(ffn_scl_step, 1)
                    dve.wait_ge(ffn_scl_step, 4 * m + k)

                dve.wait_ge(w_abs_part, N_ABS * m + ABS_ACT)
                if m == 0:
                    dve.wait_ge(w_abs_dve, N_ABS - ABS_ACT)
                nc.vector.tensor_reduce(w_all[:, 4 + m:5 + m], w_part[:, N_ABS * m:N_ABS * (m + 1)], AX_X, ALU.add).then_inc(w_abs_ready, 1)
                dve.wait_ge(w_abs_all, m + 1)
                gamma = col(G_FC + m)
                step(1, nc.vector.tensor_scalar(gamma, gamma, 1.0 / (F * D), None, ALU.mult))
                step(2, nc.vector.tensor_scalar(col(THR + m), gamma, BIT_EPS, 0.5, ALU.add, ALU.mult))
                if m == 0:
                    step(3, nc.vector.reciprocal(col(INV_G), gamma))
                    step(4, nc.vector.scalar_tensor_tensor(col(BIT_EPS_G), col(INV_G), BIT_EPS, col(INV_G), ALU.mult, ALU.mult))
                else:
                    step(3, nc.vector.tensor_scalar(col(HALF_GP), gamma, 0.5, None, ALU.mult))
                nc.vector.tensor_scalar(col(MTHR + m), col(THR + m), -1.0, None, ALU.mult).then_inc(thresholds, 1)
                dve.wait_ge(thresholds, m + 1)

            def ternary(u):
                k, m, parts = u - n_first, int(units[u][0] == "proj"), raw_parts(units[u])
                nc.vector.tensor_scalar(below[:, 2 * k % 8, :], parts[0], col(MTHR + m), None, ALU.is_lt).then_inc(w_below_dve, 1)
                dve.wait_ge(w_turned, u - 3 if k >= 4 else n_first)
                dve.wait_ge(w_below_pool, k + 1)
                nc.vector.scalar_tensor_tensor(ring(u)[:, 1, :], parts[1], col(THR + m), below[:, (2 * k + 1) % 8, :],
                                               ALU.is_gt, ALU.subtract)
                dve.wait_ge(w_below_dve, k + 1)
                nc.vector.scalar_tensor_tensor(ring(u)[:, 0, :], parts[0], col(THR + m), below[:, 2 * k % 8, :],
                                               ALU.is_gt, ALU.subtract).then_inc(w_unit_ready, 1)

            def out_weights():
                largest(3)
                dve.wait_ge(w_max_all, 4)
                attn_step(8, nc.vector.tensor_scalar(col(S_O), col(S_O), 1e-30, None, ALU.max))
                attn_step(9, nc.vector.tensor_tensor(col(SVO), col(S_V), col(S_O), ALU.mult))
                attn_step(10, nc.vector.reciprocal(col(INV + 3), col(S_O)))
                for u in range(n_first + n_tern, n_units):
                    split_weights(u)

            def first_weights():
                largest(2)
                statistics(0)
                for k, m in enumerate((2, 0, 1)):
                    if k == 1:
                        largest(0)
                        largest(1)
                    dve.wait_ge(w_max_all, k + 1)
                    attn_step(2 * k + 1, nc.vector.tensor_scalar(col(m), col(m), 1e-30 if m == 2 else 1e-12, None, ALU.max))
                    attn_step(2 * k + 2, nc.vector.reciprocal(col(INV + m), col(m)))
                    for u in range(k * ND, (k + 1) * ND):
                        split_weights(u)
                attn_step(7, nc.vector.scalar_tensor_tensor(col(EXP_SCALE), col(S_Q), DK ** -0.5 / ROPE_SHRINK ** 2, col(S_K),
                                                            ALU.mult, ALU.mult))
                width = F * D // P // N_ABS
                dve.wait_ge(w_dma[4], 16)
                for k in range(ABS_ACT, N_ABS):
                    nc.vector.tensor_reduce(w_part[:, k:k + 1], raw_fc.rearrange("p c d -> p (c d)")[:, k * width:(k + 1) * width],
                                            AX_X, ALU.add, apply_absolute_value=True).then_inc(w_abs_dve, 1)

            def token_statistics(b, t):
                if t == 0:
                    dve.wait_ge(x_dma, b * 16 + 16)
                nc.vector.bn_stats(bn[:, t, :], x_sb[:, t, :]).then_inc(bn_ready, 1)

            def join_statistics(b):
                dve.wait_ge(bn_ready, b * NT + NT)
                alone(dve)
                for t in range(NT):
                    nc.vector.bn_aggr(mean_var[:, t, :], bn[:, t, :]).then_inc(mv_ready, 1)

            def statistics(b):
                for t in range(NT):
                    token_statistics(b, t)
                join_statistics(b)

            def split_parts(parts, value, factor, ready, count, done):
                def step(k, ins):
                    ins.then_inc(ready, 1)
                    dve.wait_ge(ready, count + k)

                step(1, nc.vector.tensor_scalar(parts[:, :, 0, :], value, factor, None, ALU.mult))
                step(2, nc.vector.scalar_tensor_tensor(part_rest[:], value, factor, parts[:, :, 0, :], ALU.mult, ALU.subtract))
                step(3, nc.vector.tensor_copy(parts[:, :, 1, :], part_rest[:]))
                nc.vector.tensor_tensor(parts[:, :, 2, :], part_rest[:], parts[:, :, 1, :], ALU.subtract).then_inc(done, 1)

            def scale_by_gate(b, sums, final=False):
                dve.wait_ge(rope_sum_ready, sums)
                if final:
                    dve.wait_ge(gate_ready, b * NT + NT)
                for t in range(NT):
                    dve.wait_ge(wo_ps, b * NT + t + 1)
                    nc.vector.scalar_tensor_tensor(result[:, t, :], banks[:, t if final else 6 + t % 2, :], gate_scale[:, 1, t:t + 1],
                                                   gate[:, t, :], ALU.mult, ALU.mult).then_inc(scaled_ready, 1)

            def normalise(b):
                dve.wait_ge(ln_ready, b + 1)
                for t in range(NT):
                    nc.vector.tensor_scalar(xhat[:, t, :], x_sb[:, t, :], ln[:, 6, t:t + 1], ln[:, 7, t:t + 1],
                                            ALU.mult, ALU.add).then_inc(xhat_ready, 1)

            def split_tokens(b, first=False):
                for t in range(NT):
                    dve.wait_ge(xhi_ready, b * NT + t + 1)
                    tile = xT[:, :, :, t * P:(t + 1) * P]
                    nc.vector.tensor_tensor(tile[:, 1], banks[:, X_BANKS[t], :].rearrange("p (c n) -> p c n", c=ND), tile[:, 0],
                                            ALU.subtract).then_inc(xlo_ready, 1)
                if first:
                    dve.wait_ge(tab_dma, 32)
                dve.wait_ge(rows_dma, b * 16 + 16)
                for k in (1, 0):
                    nc.vector.tensor_tensor(rope_row[:, k, :], norm_rows, rope_tab[:, k, :], ALU.mult).then_inc(rope_row_ready, 1)

            def body(b, first=False, last=False):
                if first:
                    ffn_scales(0)
                    for u in MADE_BEFORE_ROPE:
                        ternary(u)
                dve.wait_ge(rope_row_ready, b * 2 + 2)
                for pair in range(4):
                    if pair == 0 and not first:
                        dve.wait_ge(gate_ready, b * NT)
                    if pair >= 1:
                        dve.wait_ge(rope_sum_ready, b * 8 + 2 * pair)
                    dve.wait_ge(qk_ps, b * 8 + 2 * pair + 2)
                    for k, (half, table) in enumerate(((0, 0), (1, 1), (0, 1), (1, 0))):
                        nc.vector.tensor_tensor(rope_prods[:, k, :], banks[:, 2 + 2 * (pair % 2) + half, :], rope_row[:, table, :],
                                                ALU.mult).then_inc(rope_prod_ready, 1)
                    if pair >= 2:
                        dve.wait_ge(rot_lo_ready, b * 8 + 2 * (pair - 2) + 2)
                    dve.wait_ge(rope_prod_ready, b * 16 + 4 * pair + 4)
                    for half, op in enumerate((ALU.subtract, ALU.add)):
                        nc.vector.tensor_tensor(rope_sum[:, pair % 2, half, :], rope_prods[:, 2 * half, :], rope_prods[:, 2 * half + 1, :],
                                                op).then_inc(rope_sum_ready, 1)
                    for u in MADE_AFTER_ROPE[pair] if first else []:
                        ternary(u)
                    if pair == 0 and first:
                        ffn_scales(1)
                if not first:
                    scale_by_gate(b - 1, b * 8 + 8)
                def left_blocks(r):
                    i, h0, n = ROUNDS[r]
                    dve.wait_ge(s_ps, b * NR + r + 1)
                    if i > 0:
                        src = banks[:, S_BANKS[r % NSB], 0:n * (i + 1) * P].rearrange("p (h k) -> p h k", h=n)
                        nc.vector.tensor_reduce(left_max[:, i, h0:h0 + n], src[:, :, 0:i * P], AX_X, ALU.max).then_inc(left_ready, 1)

                def diagonal_blocks(r):
                    i, h0, n = ROUNDS[r]
                    if i > 0:
                        dve.wait_ge(left_ready, b * N_LEFT + r + 1)
                    alone(dve)
                    for k in range(n):
                        at = (k * (i + 1) + i) * P
                        block = banks[:, S_BANKS[r % NSB], at:at + P]
                        ins = nc.vector.tensor_tensor_reduce(block, block, mask_q[:], 1.0, left_max[:, i, h0 + k:h0 + k + 1] if i > 0 else MASKED,
                                                             ALU.add, ALU.max, row_max[:, i, h0 + k:h0 + k + 1])
                    ins.then_inc(max_ready, 1)

                def maxima(r):
                    if r < NR:
                        left_blocks(r)
                    r = r - 1
                    if r >= 0:
                        diagonal_blocks(r)
                    if 0 <= r < BIAS_DVE:
                        i, h0, n = ROUNDS[r]
                        dve.wait_ge(max_ready, b * NR + r + 1)
                        nc.vector.tensor_scalar(exp_bias[:, i, h0:h0 + n], row_max[:, i, h0:h0 + n], col(EXP_SCALE), -1.0,
                                                ALU.mult, ALU.mult).then_inc(exp_bias_dve, 1)

                if first:
                    dve.wait_ge(w_unit_ready, n_first + n_tern)
                for f in range(FC):
                    dve.wait_ge(gelu_ready, b * FC + f + 1)
                    nc.vector.tensor_scalar(hid[:, 0, f, :], gelu_out[:, f % 4, :], col(INV_G), None, ALU.mult).then_inc(hid_hi_ready, 1)
                    dve.wait_ge(hid_hi_ready, b * FC + f + 1)
                    nc.vector.scalar_tensor_tensor(hid[:, 1, f, :], gelu_out[:, f % 4, :], col(INV_G), hid[:, 0, f, :],
                                                   ALU.mult, ALU.subtract).then_inc(hid_lo_ready, 1)
                    if f in STATS_AFTER and not first and not last:
                        token_statistics(b + 1, STATS_AFTER.index(f))
                    if f == FC - EARLY - 1 and not first and not last:
                        join_statistics(b + 1)
                    if f >= FC - EARLY:
                        maxima(f - (FC - EARLY))
                for r in range(EARLY, NR + 1):
                    maxima(r)
                dve.wait_ge(max_ready, b * NR + NR)
                split_parts(max_parts, row_max[:], -1.0, max_step, b * 3, max_split)
                if not first:
                    dve.wait_ge(max_dma, b * 16)
                dve.wait_ge(maxT_ps, b + 1)
                nc.vector.tensor_copy(maxT[:, :], banks16[0:SPLITS * H, 1, 0:S]).then_inc(maxT_ready, 1)
                mean, ex2 = ffn[:, 0, :], ffn[:, 1, :]
                neg_mean, msq, var, var_eps = (ffn[:, k, :] for k in range(2, 6))
                var_inv, nan_if_0, rstd, half_scale = (ffn[:, k, :] for k in range(6, 10))
                dve.wait_ge(sq_ps, b + 1)
                nc.vector.tensor_scalar(ffn[:, 0:2, :].rearrange("p k t -> p (k t)"), banks[:, 0, 0:2 * NT], 1.0 / F, None,
                                        ALU.mult).then_inc(sums_read, 1)
                dve.wait_ge(sums_read, b + 1)
                if first:
                    out_weights()
                n_step = 7

                def step(k, ins):
                    ins.then_inc(ffn_step, 1)
                    dve.wait_ge(ffn_step, b * n_step + k)

                step(1, nc.vector.tensor_tensor(msq, mean, mean, ALU.mult))
                step(2, nc.vector.tensor_tensor(var, ex2, msq, ALU.subtract))
                nc.vector.tensor_scalar(var_eps, var, col(BIT_EPS_G), None, ALU.add).then_inc(var_ready, 1)
                step(3, nc.vector.tensor_scalar(neg_mean, mean, -1.0, None, ALU.mult))
                step(4, nc.vector.reciprocal(var_inv, var))
                step(5, nc.vector.tensor_tensor(nan_if_0, var, var_inv, ALU.mult))
                dve.wait_ge(rstd_ready, b + 1)
                step(6, nc.vector.scalar_tensor_tensor(gate_scale[:, 0, :], rstd, col(HALF_GP), nan_if_0, ALU.mult, ALU.mult))
                step(7, nc.vector.tensor_scalar(gate_scale[:, 1, :], gate_scale[:, 0, :], col(SVO), None, ALU.mult))
                dve.wait_ge(sum_ready, b * NR + NR)
                dve.wait_ge(max_split, b + 1)
                alone(dve)
                nc.vector.reciprocal(row_sum[:], row_sum[:]).then_inc(inv_ready, 1)
                dve.wait_ge(inv_ready, b + 1)
                split_parts(inv_parts, row_sum[:], INV_GROW, inv_step, b * 3, inv_split)
                for t in range(NT):
                    if t == NT - 1:
                        dve.wait_ge(invT_ps, b + 1)
                        nc.vector.tensor_copy(invT, banks16[0:SPLITS * H, 6, 0:S]).then_inc(invT_ready, 1)
                    if t < 2:
                        dve.wait_ge(down_kept, b * 2 + t + 1)
                    else:
                        dve.wait_ge(down_ps, b * NT + t + 1)
                    nc.vector.scalar_tensor_tensor(gate[:, t, :], w_rowsum[:], neg_mean[:, t:t + 1],
                                                   gate[:, t, :] if t < 2 else banks[:, 6 + t % 2, :],
                                                   ALU.mult, ALU.add).then_inc(centred, 1)
                if first:
                    statistics(1)

                def finish_context(g):
                    if g >= 2:
                        dve.wait_ge(ctx_lo, b * NG + g - 1)
                    if g >= 1:
                        dve.wait_ge(ctx_ready, b * NG + g)
                    dve.wait_ge(spread_ps, b * NG + g + 1)
                    nc.vector.tensor_copy(inv_spread, banks[:, 7, :]).then_inc(spread_kept, 1)
                    dve.wait_ge(spread_kept, b * NG + g + 1)
                    dve.wait_ge(pv_ps, b * NG + g + 1)
                    nc.vector.tensor_tensor(ctx_f32[:, g % 2, :], banks[:, 6, :], inv_spread, ALU.mult).then_inc(ctx_ready, 1)

                def finish_gate(t):
                    dve.wait_ge(tanh_ready, b * NT + t + 1)
                    nc.vector.scalar_tensor_tensor(gate[:, t, :], tanh_sb[:, t, :], 1.0, gate[:, t, :],
                                                   ALU.add, ALU.mult).then_inc(gate_ready, 1)

                for g in range(NG):
                    if g == (2 if first else 0) and not last:
                        normalise(b + 1)
                    finish_context(g)
                    if g == 2 and not last:
                        split_tokens(b + 1)
                for t in range(NT):
                    finish_gate(t)

            first_weights()
            split_tokens(0, first=True)
            body(0, first=True)
            with dve.Fori(1, NB - 1) as b:
                body(b)
            body(NB - 1, last=True)
            scale_by_gate(NB - 1, NB * 8, final=True)

        @block.gpsimd
        def _(pool):
            nc.gpsimd.memset(ones32[:], 1.0)
            nc.gpsimd.memset(ones16[:], 1.0)
            nc.gpsimd.memset(ident16[:], 0.0)
            nc.gpsimd.memset(ident32[:], 0.0)
            nc.gpsimd.memset(mask_q[:], 0.0)
            nc.gpsimd.memset(selector[:], 0.0)
            nc.gpsimd.memset(minus_half[:], -0.5).then_inc(ln_step, 1)
            pool.wait_ge(ln_step, 1)
            for ident in (ident16, ident32):
                nc.gpsimd.affine_select(ident[:], ident[:], [[-1, P]], ALU.not_equal, 1.0, base=0, channel_multiplier=1)
            for part in range(SPLITS):
                if part:
                    pool.wait_ge(selector_step, part)
                nc.gpsimd.affine_select(selector[:], selector[:], [[-1, H], [0, DK]], ALU.not_equal, 1.0 / INV_GROW,
                                        base=-H * part, channel_multiplier=1).then_inc(selector_step, 1)
            nc.gpsimd.affine_select(mask_q[:], mask_q[:], [[-1, P]], ALU.is_ge, MASKED, base=0, channel_multiplier=1).then_inc(consts, 1)
            LN_STEPS = 9

            def normalise(b, first=False):
                mean, var = mean_var[:, :, 0], mean_var[:, :, 1]
                a1, r1, sq, v2, a2, r2, rr, shift = (ln[:, k, :] for k in range(8))

                def step(k, ins):
                    ins.then_inc(ln_step, 1)
                    pool.wait_ge(ln_step, b * LN_STEPS + 1 + k)
                    alone(pool)

                pool.wait_ge(mv_ready, b * NT + NT)
                if not first:
                    pool.wait_ge(v_ready, b * NT)
                    pool.wait_ge(rows_dma, b * 16)
                alone(pool)
                step(1, nc.gpsimd.tensor_scalar(a1, var, LN_EPS, None, ALU.add))
                step(2, nc.gpsimd.tensor_tensor(r1, a1, minus_half[:], ALU.pow))
                step(3, nc.gpsimd.tensor_tensor(sq, r1, r1, ALU.mult))
                step(4, nc.gpsimd.tensor_tensor(v2, sq, var, ALU.mult))
                step(5, nc.gpsimd.tensor_scalar(a2, v2, BIT_EPS, None, ALU.add))
                step(6, nc.gpsimd.tensor_tensor(r2, a2, minus_half[:], ALU.pow))
                step(7, nc.gpsimd.tensor_tensor(rr, r1, r2, ALU.mult))
                step(8, nc.gpsimd.tensor_tensor(shift, mean, rr, ALU.mult))
                step(9, nc.gpsimd.tensor_tensor(norm_c[:], a2, r2, ALU.mult))
                nc.gpsimd.tensor_scalar(shift, shift, -1.0, None, ALU.mult).then_inc(ln_ready, 1)

            def add_x(b):
                for t in range(NT):
                    pool.wait_ge(resid_dma[t % 2], b * 32 + 16 * (t // 2) + 16)
                    pool.wait_ge(scaled_ready, b * NT + t + 1)
                    nc.gpsimd.tensor_tensor(result[:, t, :], result[:, t, :], resid[:, t % 2, :], ALU.add).then_inc(result_ready, 1)

            def body(b, first=False, last=False):
                if first:
                    magnitudes_all(0)
                    for u in BELOW_BEFORE_ROPE:
                        below_threshold(u)
                for pair in range(4):
                    for half in range(2):
                        pool.wait_ge(rot_hi_ready, b * 8 + 2 * pair + half + 1)
                        nc.gpsimd.tensor_tensor(split_buf[:, pair % 2, 2 + half, :], rope_sum[:, pair % 2, half, :],
                                                split_buf[:, pair % 2, half, :], ALU.subtract).then_inc(rot_lo_ready, 1)
                    for u in BELOW_AFTER_ROPE[pair] if first else []:
                        if u == n_first + FC // 2:
                            magnitudes_all(1)
                        below_threshold(u)
                if not first:
                    add_x(b - 1)
                for f in range(1, FC):
                    pool.wait_ge(sq_ready, b * FC + f + 1)
                    if f >= 2:
                        pool.wait_ge(sq_added, b * (FC - 1) + f - 1)
                    nc.gpsimd.tensor_tensor(sq_sum[:], sq_sum[:], squares[:, f % 2, :], ALU.add).then_inc(sq_added, 1)
                for r, (i, h0, n) in list(enumerate(ROUNDS))[BIAS_DVE:]:
                    pool.wait_ge(max_ready, b * NR + r + 1)
                    alone(pool)
                    nc.gpsimd.tensor_scalar(exp_bias[:, i, h0:h0 + n], row_max[:, i, h0:h0 + n], col(EXP_SCALE), -1.0, ALU.mult, ALU.mult
                                            ).then_inc(exp_bias_ready, 1)
                if first:
                    largest_all(3, 3)
                elif not last:
                    normalise(b + 1)
                pool.wait_ge(var_ready, b + 1)
                nc.gpsimd.tensor_tensor(ffn[:, 8, :], ffn[:, 5, :], minus_half[:], ALU.pow).then_inc(rstd_ready, 1)

                def mask(g, heads=range(GH)):
                    for k in heads:
                        pool.wait_ge(probs_ready, b * H + GH * g + k + 1)
                        alone(pool)
                        head = probs[:, g % 2, k, :]
                        for blocks in (head[:, 0:1024].rearrange("p (j c) -> p j c", c=512)[:, :, 0:P],
                                       head[:, KEY_COLS[3]:KEY_COLS[3] + 2 * P].rearrange("p (j c) -> p j c", c=P)):
                            nc.gpsimd.affine_select(blocks, blocks, [[0, 2], [1, P]], ALU.is_ge, 0.0, base=0,
                                                    channel_multiplier=-1).then_inc(probs_masked, 1)

                def split_context(g):
                    pool.wait_ge(ctx_hi, b * NG + g + 1)
                    nc.gpsimd.tensor_tensor(ctxT[:, 1, g, :], ctx_f32[:, g % 2, :], ctxT[:, 0, g, :], ALU.subtract).then_inc(ctx_lo, 1)

                mask(0)
                mask(1)
                if first:
                    normalise(b + 1)
                for g in range(2, NG):
                    mask(g, range(GH // 2))
                    split_context(g - 2)
                    mask(g, range(GH // 2, GH))
                for g in range(NG - 2, NG):
                    split_context(g)

            def largest_all(k, m):
                pool.wait_ge(w_max_ready, k + 1)
                nc.gpsimd.partition_all_reduce(col(m), w_all[:, m:m + 1], P, RMAX).then_inc(w_max_all, 1)

            def magnitudes_all(m):
                pool.wait_ge(w_abs_ready, m + 1)
                nc.gpsimd.partition_all_reduce(col(G_FC + m), w_all[:, 4 + m:5 + m], P, RADD).then_inc(w_abs_all, 1)
                pool.wait_ge(thresholds, m + 1)

            def below_threshold(u):
                k, m = u - n_first, int(units[u][0] == "proj")
                if k >= 4:
                    pool.wait_ge(w_unit_ready, u - 3)
                nc.gpsimd.tensor_scalar(below[:, (2 * k + 1) % 8, :], raw_parts(units[u])[1], col(MTHR + m), None,
                                        ALU.is_lt).then_inc(w_below_pool, 1)

            largest_all(0, 2)
            normalise(0, first=True)
            largest_all(1, 0)
            largest_all(2, 1)
            body(0, first=True)
            with pool.Fori(1, NB - 1) as b:
                body(b)
            body(NB - 1, last=True)
            add_x(NB - 1)


_INS = ["L0_attn_x", "L0_attn_Wq", "L0_attn_Wk", "L0_attn_Wv", "L0_attn_Wo", "L0_ffn_w_fc", "L0_ffn_w_proj"]


def rope_tables():
    import numpy as np

    inv_freq = np.exp(np.float32(-np.log(10000.0)) * np.arange(0, DK, 2, dtype=np.float32) / np.float32(DK))
    angle = np.arange(S, dtype=np.float32)[None, :] * np.repeat(inv_freq.astype(np.float32), HS)[:, None]
    return [np.ascontiguousarray(f(angle).astype(np.float32) * np.float32(ROPE_SHRINK)) for f in (np.cos, np.sin)]


def kernel(**inputs):
    import numpy as _np
    import concourse.bacc as _bacc
    from concourse import mybir as _mybir
    from concourse.bass_utils import run_bass_kernel_spmd as _run

    nc = _bacc.Bacc("TRN2", target_bir_lowering=False, num_devices=1)
    arrays, args = {}, []
    named = [(name, _np.ascontiguousarray(inputs[name])) for name in _INS]
    named += list(zip(("rope_cos", "rope_sin"), rope_tables()))
    for name, a in named:
        arrays[f"in_{name}_dram"] = a
        args.append(nc.dram_tensor(f"in_{name}_dram", a.shape, _mybir.dt.from_np(a.dtype), kind="ExternalInput").ap())
    args.append(nc.dram_tensor("out_0_dram", (NB, S, D), F32, kind="ExternalOutput").ap())
    args.append(nc.dram_tensor("norm_row", (S,), F32, kind="Internal").ap())
    program(nc, *args)
    r = _run(nc, [arrays], core_ids=[0])
    return r.results[0]["out_0_dram"]
```
